# Optimizing a Trainium2 kernel written in Bass

```python
import numpy as np
import jax
import jax.numpy as jnp

def _softmax(x, axis=-1):
    return jax.nn.softmax(x, axis=axis)

def _gelu(x):
    return jax.nn.gelu(x, approximate=True)

def _silu(x):
    return jax.nn.silu(x)

def _sigmoid(x):
    return jax.nn.sigmoid(x)

def _layernorm(x, axis=-1, eps=1e-05):
    m = jnp.mean(x, axis=axis, keepdims=True)
    v = jnp.var(x, axis=axis, keepdims=True)
    return (x - m) / jnp.sqrt(v + eps)

def _scatter_add(tgt, idx, src, axis=0):
    return tgt.at[idx].add(src)

def _segment_sum(src, seg, n):
    return jax.ops.segment_sum(src, seg, n)
kernel_name = 'mk_adj_seq_d2_adj_r2_d8b535'

def setup_inputs(seed: int=0):
    np.random.seed(seed)
    _w = jnp.asarray

    def _rec_inputs():
        import jax
        import jax.numpy as jnp
        _gk = jax.random.key(seed)
        x = -0.0002928 + 1 * jax.random.normal(jax.random.fold_in(_gk, 1), (16, 512, 256), jnp.float32)
        _a = jax.random.bernoulli(jax.random.fold_in(_gk, 2), 0.015625, (16, 512, 512))
        _af = _a.astype(jnp.float32)
        adj = _af
        return (x, adj)
    x, adj = _rec_inputs()

    def _L0_gnn_setup():
        import jax, jax.numpy as jnp
        import numpy as np
        D_MODEL = 256
        N_HEADS = 8
        D_HEAD = D_MODEL // N_HEADS
        B = 8
        N = 512
        EPS = 1e-05
        key = jax.random.key(seed)
        ks = jax.random.split(key, 12)
        x = jax.random.normal(ks[0], (B, N, D_MODEL), dtype=jnp.float32)
        adj = (jax.random.uniform(ks[1], (B, N, N)) < 0.05).astype(jnp.float32)
        s = 1.0 / np.sqrt(D_MODEL)

        def lin(kw, kb):
            W = jax.random.uniform(kw, (D_MODEL, D_MODEL), minval=-s, maxval=s, dtype=jnp.float32)
            b = jax.random.uniform(kb, (D_MODEL,), minval=-s, maxval=s, dtype=jnp.float32)
            return (W, b)
        Wq, bq = lin(ks[2], ks[3])
        Wk, bk = lin(ks[4], ks[5])
        Wv, bv = lin(ks[6], ks[7])
        Wo, bo = lin(ks[8], ks[9])
        gamma = jnp.ones((D_MODEL,), dtype=jnp.float32)
        beta = jnp.zeros((D_MODEL,), dtype=jnp.float32)
        return {'x': x, 'adj': adj, 'Wq': Wq, 'bq': bq, 'Wk': Wk, 'bk': bk, 'Wv': Wv, 'bv': bv, 'Wo': Wo, 'bo': bo, 'gamma': gamma, 'beta': beta}
    _L0_gnn_all = _L0_gnn_setup()
    _L0_gnn_in = {k: v for k, v in _L0_gnn_all.items() if k in ('Wq', 'bq', 'Wk', 'bk', 'Wv', 'bv', 'Wo', 'bo', 'gamma', 'beta')}
    del _L0_gnn_all

    def _L1_gnn_setup():
        import jax, jax.numpy as jnp
        import numpy as np
        BS, N, H = (8, 1024, 256)
        NEG_INF = -1000000000.0
        LEAKY_SLOPE = 0.01
        key = jax.random.key(seed)
        ks = jax.random.split(key, 8)
        feats = jax.random.normal(ks[0], (BS, N, H), dtype=jnp.float32)
        adj = jax.random.randint(ks[1], (BS, N, N), 0, 2).astype(jnp.float32)
        adj = jnp.maximum(adj, jnp.eye(N, dtype=jnp.float32)[None])
        s = 1.0 / np.sqrt(H)
        return {'feats': feats, 'adj_mat': adj, 'fc_w': jax.random.normal(ks[2], (H, H), dtype=jnp.float32) * s, 'fc_b': jax.random.normal(ks[3], (H,), dtype=jnp.float32) * s, 'q_w': jax.random.normal(ks[4], (1, H), dtype=jnp.float32) * s, 'q_b': jax.random.normal(ks[5], (1,), dtype=jnp.float32) * s, 'k_w': jax.random.normal(ks[6], (1, H), dtype=jnp.float32) * s, 'k_b': jax.random.normal(ks[7], (1,), dtype=jnp.float32) * s}
    _L1_gnn_all = _L1_gnn_setup()
    _L1_gnn_in = {k: v for k, v in _L1_gnn_all.items() if k in ('fc_w', 'fc_b', 'q_w', 'q_b', 'k_w', 'k_b')}
    del _L1_gnn_all
    return {'x': x, 'adj': adj, 'L0_gnn_Wq': _L0_gnn_in['Wq'], 'L0_gnn_bq': _L0_gnn_in['bq'], 'L0_gnn_Wk': _L0_gnn_in['Wk'], 'L0_gnn_bk': _L0_gnn_in['bk'], 'L0_gnn_Wv': _L0_gnn_in['Wv'], 'L0_gnn_bv': _L0_gnn_in['bv'], 'L0_gnn_Wo': _L0_gnn_in['Wo'], 'L0_gnn_bo': _L0_gnn_in['bo'], 'L0_gnn_gamma': _L0_gnn_in['gamma'], 'L0_gnn_beta': _L0_gnn_in['beta'], 'L1_gnn_fc_w': _L1_gnn_in['fc_w'], 'L1_gnn_fc_b': _L1_gnn_in['fc_b'], 'L1_gnn_q_w': _L1_gnn_in['q_w'], 'L1_gnn_q_b': _L1_gnn_in['q_b'], 'L1_gnn_k_w': _L1_gnn_in['k_w'], 'L1_gnn_k_b': _L1_gnn_in['k_b']}

def reference(x, adj, L0_gnn_Wq, L0_gnn_bq, L0_gnn_Wk, L0_gnn_bk, L0_gnn_Wv, L0_gnn_bv, L0_gnn_Wo, L0_gnn_bo, L0_gnn_gamma, L0_gnn_beta, L1_gnn_fc_w, L1_gnn_fc_b, L1_gnn_q_w, L1_gnn_q_b, L1_gnn_k_w, L1_gnn_k_b):
    import jax
    import jax.numpy as jnp

    def _L0_gnn_ref(x, adj, Wq, bq, Wk, bk, Wv, bv, Wo, bo, gamma, beta):
        import jax, jax.numpy as jnp
        import numpy as np
        D_MODEL = 256
        N_HEADS = 8
        D_HEAD = D_MODEL // N_HEADS
        B = 8
        N = 512
        EPS = 1e-05
        Bsz, n, _ = x.shape

        def proj(W, b):
            y = x @ W.T + b
            return y.reshape(Bsz, n, N_HEADS, D_HEAD).transpose(0, 2, 1, 3)
        q, k, v = (proj(Wq, bq), proj(Wk, bk), proj(Wv, bv))
        scores = jnp.einsum('bhqd,bhkd->bhqk', q, k) / np.sqrt(D_HEAD)
        mask = adj + jnp.eye(n, dtype=adj.dtype)[None] > 0
        scores = jnp.where(mask[:, None], scores, -jnp.inf)
        attn = jax.nn.softmax(scores, axis=-1)
        out = jnp.einsum('bhqk,bhkd->bhqd', attn, v)
        out = out.transpose(0, 2, 1, 3).reshape(Bsz, n, D_MODEL)
        out = out @ Wo.T + bo
        h = x + out
        mu = jnp.mean(h, axis=-1, keepdims=True)
        var = jnp.mean(jnp.square(h - mu), axis=-1, keepdims=True)
        return (h - mu) * jax.lax.rsqrt(var + EPS) * gamma + beta

    def _L1_gnn_ref(feats, adj_mat, fc_w, fc_b, q_w, q_b, k_w, k_b):
        import jax, jax.numpy as jnp
        import numpy as np
        BS, N, H = (8, 1024, 256)
        NEG_INF = -1000000000.0
        LEAKY_SLOPE = 0.01
        feat_proj = jnp.einsum('bnh,oh->bno', feats, fc_w) + fc_b
        q = jnp.einsum('bnh,oh->bno', feat_proj, q_w) + q_b
        k = jnp.einsum('bnh,oh->bno', feat_proj, k_w) + k_b
        logits = q + jnp.swapaxes(k, 2, 1)
        masked = logits + (1.0 - adj_mat) * NEG_INF
        masked = jnp.where(masked >= 0, masked, LEAKY_SLOPE * masked)
        atten = jax.nn.softmax(masked, axis=-1)
        out = jnp.einsum('bnm,bmh->bnh', atten, feat_proj)
        return out + feats
    x = _L0_gnn_ref(x, adj, L0_gnn_Wq, L0_gnn_bq, L0_gnn_Wk, L0_gnn_bk, L0_gnn_Wv, L0_gnn_bv, L0_gnn_Wo, L0_gnn_bo, L0_gnn_gamma, L0_gnn_beta)
    x = _L1_gnn_ref(x, adj, L1_gnn_fc_w, L1_gnn_fc_b, L1_gnn_q_w, L1_gnn_q_b, L1_gnn_k_w, L1_gnn_k_b)
    return x

_drawn_inputs = setup_inputs


def setup_inputs(seed=0):
    import zlib

    import numpy as np

    out = dict(_drawn_inputs(seed))
    spreads = {'L0_gnn_gamma': (1.0, 0.2), 'L0_gnn_beta': (0.0, 0.1)}
    factors = {'L0_gnn_bq': 24.147, 'L0_gnn_bk': 64.0}
    for name, (base, spread) in spreads.items():
        noise = np.random.default_rng([zlib.crc32(name.encode()), seed]).standard_normal(out[name].shape)
        drawn = base * np.exp(spread * noise) if base else spread * noise
        out[name] = jnp.asarray(drawn.astype(out[name].dtype))
    for name, factor in factors.items():
        out[name] = (out[name] * factor).astype(out[name].dtype)
    return out
```

```python
from contextlib import ExitStack

import concourse.bass as bass
from concourse import mybir

F32 = mybir.dt.float32
F32R = mybir.dt.float32r
BF16 = mybir.dt.bfloat16
ALU = mybir.AluOpType
ACT = mybir.ActivationFunctionType
AX = mybir.AxisListType

P = 128
NB, N, D = 16, 512, 256
NH, DH = 8, 32
GH = P // DH
NG = NH // GH
NT = N // P
DT = D // P
POS = NG * NT * GH
SCALE = float(DH) ** -0.5
BIG = 2.0 ** 100
NEG_INF = -1e9
SLOPE = 0.01
EPS = 1e-5
LOWEST = -3.0e38
STACK = 3 * DH
LEAD = 20

FIRST, LOOP_FROM, LOOP_TO, LAST = -1, 4, 14, NB + 1


def on(t, off):
    return not isinstance(t, int) or 0 <= t + off < NB


class Signal:

    def __init__(self, sem, steps, by=1):
        self.sem, self.by = sem, by
        self.place = {name: n for n, (name, _) in enumerate(steps)}
        self.offs = [off for _, off in steps]
        assert len(self.place) == len(steps)

    def after(self, step, t):
        last = self.place[step]
        if isinstance(t, int):
            return self.by * sum(min(max(t + off + (n <= last), 0), NB) for n, off in enumerate(self.offs))
        return t * (self.by * len(self.offs)) + self.by * sum(off + (n <= last) for n, off in enumerate(self.offs))


PE_STEPS = [
    (0, "xt0", 1), (1, "xt1", 1), (1, "m4", 0), (2, "pv0", -1), (3, "q0", 1),
    (4, "k0", 1), (4, "et0", -2), (5, "m5", 0), (6, "pv1", 0), (6, "et1", -2), (6, "sum1", -1), (7, "et2", -2),
    (8, "et3", -2), (9, "m6", 0), (10, "pv2", 0), (10, "at0", -2), (12, "at1", -2), (13, "m7", 0),
    (13, "op0", -1), (14, "pv3", 0), (14, "op1", -1), (15, "mt0", 1), (16, "mt1", 1), (17, "m0", 1),
    (17, "q1", 1), (18, "pv4", 0), (18, "k1", 1), (19, "v0", 1), (20, "v1", 1), (21, "m1", 1),
    (22, "pv5", 0), (22, "ht0", -1), (22, "sum0", 0), (23, "ht1", -1), (25, "m2", 1),
    (26, "pv6", 0), (26, "fc0", -1), (27, "fc1", -1), (28, "kb", -1), (29, "m3", 1), (30, "pv7", 0)]
OFF = {name: off for _, name, off in PE_STEPS}
FILLS = [name for _, name, _ in PE_STEPS if not name.startswith("pv")]
READ_BY = {
    "xt0": ("dve", "x_lo0"), "xt1": ("dve", "x_lo1"), "q0": ("dve", "q_lo0"), "k0": ("dve", "k_lo0"),
    "q1": ("dve", "q_lo1"), "k1": ("dve", "k_lo1"), "v0": ("act", "v0"), "v1": ("act", "v1"),
    "mt0": ("act", "mt0"), "mt1": ("act", "mt1"), "sum0": ("dve", "recip0b"), "sum1": ("dve", "recip1b"),
    "op0": ("dve", "h_add0"), "op1": ("dve", "h_add1"), "ht0": ("dve", "h_lo0"), "ht1": ("dve", "h_lo1"),
    "fc0": ("act", "feat0"), "fc1": ("act", "feat1"), "kb": ("dve", "l_max3"), "at0": ("dve", "fin0"),
    "at1": ("dve", "fin1"), **{f"et{c}": ("act", f"et{c}") for c in range(NT)},
    **{f"m{j}": ("dve", f"m{j}") for j in range(NH)}}
ACT_STEPS = [
    ("logit2", -2), ("logit3", -2), ("x_hi0", 1), ("lexp0", -2), ("x_hi1", 1), ("lexp1", -2), ("o_raw1", -1),
    ("q_hi0", 1), ("k_hi0", 1), ("et0", -2), ("lexp2", -2), ("lexp3", -2), ("et1", -2), ("et2", -2),
    ("et3", -2), ("o_hi1", -1), ("mt0", 1), ("mt1", 1), ("q_hi1", 1), ("k_hi1", 1), ("o_raw0", 0),
    ("v0", 1), ("v1", 1), ("h_hi0", -1), ("h_hi1", -1), ("o_hi0", 0), ("feat0", -1), ("feat1", -1),
    ("logit0", -1), ("logit1", -1)]
DVE_STEPS = [
    ("leaky0", -2), ("leaky1", -2), ("x_lo0", 1), ("leaky2", -2), ("x_lo1", 1), ("m4", 0), ("leaky3", -2), ("q_lo0", 1), ("k_lo0", 1), ("mask", 1), ("m5", 0),
    ("recip1a", -1), ("recip1b", -1), ("o_norm1", -1), ("m6", 0), ("l_recip", -2), ("fin0", -2), ("o_lo1", -1),
    ("fin1", -2), ("m7", 0), ("h_add0", -1), ("h_add1", -1), ("stats", -1), ("moments", -1), ("var_eps", -1),
    ("centre", -1), ("m0", 1), ("q_lo1", 1), ("k_lo1", 1), ("h_a", -1), ("h_b", -1), ("m1", 1),
    ("recip0a", 0), ("recip0b", 0), ("h_lo0", -1), ("h_lo1", -1), ("o_norm0", 0), ("m2", 1), ("q_dot0", -1), ("o_lo0", 0),
    ("q_dot1", -1), ("q_bias", -1), ("l_max1", -1), ("m3", 1), ("l_max3", -1), ("l_z", -1), ("l_nz", -1),
    ("l_negmax", -1)]
POOL_STEPS = [
    ("sum1_3", -1), ("x_bo", -1), ("diag", 1), ("sum0_1", 0), ("sum0_2", 0), ("rstd", -1), ("sum0_3", 0),
    ("l_mask", -1), ("sum1_1", 0), ("h_fcb", -1), ("sum1_2", 0)]


def maxima_tile(s):
    n = s - (POS - LEAD) if s >= POS - LEAD else s + LEAD
    return (1 if s >= POS - LEAD else 0), n // NT, n % NT


def build(nc, x, adj, wq, bq, wk, bk, wv, bv, wo, bo, gamma, beta, fc_w, fc_b, q_w, q_b, k_w, k_b, out):
    with ExitStack() as ctx:
        def sb(name, shape, dt=F32):
            return ctx.enter_context(nc.sbuf_tensor(name, shape, dt))

        def sem(name):
            return ctx.enter_context(nc.semaphore(name))

        weight_hi = sb("weight_hi", [P, 5, DT, D], F32R)
        weight_lo = sb("weight_lo", [P, 5, DT, D], F32R)
        WQ, WK, WV, WO, FC = range(5)
        uk_hi = sb("uk_hi", [P, DT, P], F32R)
        uk_lo = sb("uk_lo", [P, DT, P], F32R)
        bias_col = sb("bias_col", [P, 3, NG])
        gamma_row = sb("gamma_row", [P, D])
        beta_row = sb("beta_row", [P, D])
        bo_row = sb("bo_row", [P, D])
        fcb_row = sb("fcb_row", [P, D])
        qw_row = sb("qw_row", [P, D])
        kw_col = sb("kw_col", [P, DT])
        qkb = sb("qkb", [P, 2])
        logit_bias = sb("logit_bias", [P, 4])
        ident = sb("ident", [P, P])
        ident_b = sb("ident_b", [P, P], BF16)
        ones = sb("ones", [P, DH])
        minus_half = sb("minus_half", [P, NT])
        x_in = sb("x_in", [P, NT, D])
        adj_in = sb("adj_in", [P, NT, N])
        masks = sb("masks", [P, (2 * NT + 1) * N], BF16)
        mask = [masks[:, i * NT * N:(i + 1) * NT * N] for i in range(2)]
        mask_diag = [masks[:, i * NT * N:i * NT * N + NT * (N + P)].rearrange("p (c n) -> p c n", c=NT)[:, :, 0:P]
                     for i in range(2)]
        mask_t = [sb(f"mask_t{i}", [P, NT, N], BF16) for i in range(2)]
        xt_hi = sb("xt_hi", [P, DT, N], F32R)
        xt_lo = sb("xt_lo", [P, DT, N], F32R)
        qt_hi = [sb(f"qt_hi{g}", [P, N], F32R) for g in range(NG)]
        qt_lo = [sb(f"qt_lo{g}", [P, N], F32R) for g in range(NG)]
        kt_hi = [sb(f"kt_hi{g}", [P, N], F32R) for g in range(NG)]
        kt_lo = [sb(f"kt_lo{g}", [P, N], F32R) for g in range(NG)]
        q_stack = [sb(f"q_stack{g}", [STACK + 1, GH, N], F32R) for g in range(NG)]
        k_stack = [sb(f"k_stack{g}", [STACK + 1, GH, N], F32R) for g in range(NG)]
        v = [sb(f"v{i}", [P, NT, D]) for i in range(2)]
        row_max = sb("row_max", [P, NH, NT])
        neg_max = sb("neg_max", [NT, 2, P], F32R)
        e = sb("e", [P, NT, GH, N])
        e_sum = sb("e_sum", [P, GH, N])
        recip = x_in[:, 0:2, :].rearrange("p c d -> p (c d)")
        o_raw = x_in[:, 2:4, :].rearrange("p c d -> p (c d)")
        o_hi = sb("o_hi", [P, NG, N], F32R)
        o_lo = sb("o_lo", [P, NG, N], F32R)
        h = [sb(f"h{i}", [P, NT, D]) for i in range(2)]
        stats = sb("stats", [P, NT, 6])
        moments = sb("moments", [P, NT, 2])
        var_eps = sb("var_eps", [P, NT])
        rstd = sb("rstd", [P, NT])
        ht_hi = sb("ht_hi", [P, DT, N], F32R)
        ht_lo = sb("ht_lo", [P, DT, N], F32R)
        feat = sb("feat", [P, NT, D])
        z = sb("z", [P, NT, N])
        zt = sb("zt", [P, NT, N])
        q_dot = sb("q_dot", [P, NT])
        q_bias = sb("q_bias", [P, NT])
        l_max = sb("l_max", [P, NT])
        l_z = sb("l_z", [P, NT])
        l_nz = sb("l_nz", [P, NT])
        l_negmax = sb("l_negmax", [P, NT])
        l_sum = sb("l_sum", [P, NT])
        l_recip = sb("l_recip", [P, NT])

        def pb(name):
            return ctx.enter_context(nc.psum_tensor(name, [P, 512], F32))
        st_bank = [pb("st_bank0"), pb("st_bank1")]
        sm_bank = [pb("sm_bank0"), pb("sm_bank1")]
        o_bank = pb("o_bank")
        shared = [pb(f"shared{i}") for i in range(3)]
        bank_of = {name: shared[n % 3] for n, name in enumerate(FILLS)}
        before = {name: (FILLS[n - 3], n < 3) for n, name in enumerate(FILLS)}

        tiles = [(s, 0) for s in range(POS)]
        st_done = Signal(sem("st_done"), tiles)
        exp_done = Signal(sem("exp_done"), tiles)
        sm_tiles = [(s, maxima_tile(s)[0]) for s in range(POS)]
        sm_done = Signal(sem("sm_done"), sm_tiles)
        max_done = Signal(sem("max_done"), sm_tiles)
        pe_done = Signal(sem("pe_done"), [(name, off) for _, name, off in PE_STEPS])
        act_done = Signal(sem("act_done"), ACT_STEPS)
        dve_done = Signal(sem("dve_done"), DVE_STEPS)
        pool_done = Signal(sem("pool_done"), POOL_STEPS)
        made = {"act": act_done, "dve": dve_done}
        adj_loaded = Signal(sem("adj_loaded"), [("adj", 1), ("adj_again", -1)], 16)
        x_loaded = Signal(sem("x_loaded"), [("x", 2)], 16)
        h_loaded = Signal(sem("h_loaded"), [("x_again", 0)], 16)
        stacked = [Signal(sem("stacked0"), [("g0", 1)], 16 * 6 * GH), Signal(sem("stacked1"), [("g1", 0)], 16 * 6 * GH)]
        max_placed = [Signal(sem(f"max_placed{i}"), [("g1", 0), ("g0", 1)], 16) for i in range(GH)]
        stored = [Signal(sem(f"stored{i}"), [("out", -2)], 16) for i in range(2)]
        const_loaded = sem("const_loaded")
        ident_made = sem("ident_made")
        setup_pe, setup_act, setup_dve = sem("setup_pe"), sem("setup_act"), sem("setup_dve")

        def f(ap):
            return ap.bitcast(F32)

        def rows(dram, b, c0=0, c1=NT):
            return dram[bass.ds(b, 1), c0 * P:c1 * P, :].rearrange("a (c p) d -> p (a c) d", p=P)

        block = ctx.enter_context(nc.Block())

        def program(engine, iteration):
            for t in range(FIRST, LOOP_FROM):
                iteration(t, t % 2)
            with engine.Fori(LOOP_FROM // 2, LOOP_TO // 2) as pair:
                iteration(2 * pair, 0)
                iteration(2 * pair + 1, 1)
            for t in range(LOOP_TO, LAST + 1):
                iteration(t, t % 2)

        @block.sync
        def _(sp):
            n = 0
            for k, w in enumerate((wq, wk, wv, wo)):
                sp.dma_start(z[:, k, :].rearrange("p (o i) -> p o i", o=DT),
                             w.rearrange("(o p) i -> p o i", p=P)).then_inc(const_loaded, 16)
            sp.dma_start(h[0][:, 0:DT, :], fc_w.rearrange("(o p) i -> p o i", p=P)).then_inc(const_loaded, 16)
            for k, b in enumerate((bq, bk, bv)):
                sp.dma_start(bias_col[:, k, :], b.rearrange("(g p) -> p g", p=P),
                             allow_slow_non_contiguous=True).then_inc(const_loaded, 16)
            sp.dma_start(kw_col[:, :], k_w.rearrange("a (g p) -> p (a g)", p=P),
                         allow_slow_non_contiguous=True).then_inc(const_loaded, 16)
            for row, b in ((gamma_row, gamma), (beta_row, beta), (bo_row, bo), (fcb_row, fc_b)):
                sp.dma_start(row[:, :], b.partition_broadcast(P)).then_inc(const_loaded, 16)
            for row, b in ((qw_row[:, :], q_w), (zt[:, 2, 0:D], k_w)):
                sp.dma_start(row, b.rearrange("a d -> (a d)").partition_broadcast(P)).then_inc(const_loaded, 16)
            for k, b in enumerate((q_b, k_b)):
                sp.dma_start(qkb[:, k:k + 1], b.partition_broadcast(P)).then_inc(const_loaded, 16)
            sp.dma_start(x_in[:, :, :], rows(x, 0)).then_inc(x_loaded.sem, 16)

            def stack(g, t):
                sp.wait_ge(dve_done.sem, dve_done.after(f"k_lo{g}", t if g == 0 else t - 1))
                sp.nop(nofuse=True)
                for i in range(GH):
                    r = slice(DH * i, DH * (i + 1))
                    for part, (q_part, k_part) in enumerate(((qt_hi, kt_hi), (qt_lo, kt_hi), (qt_hi, kt_lo))):
                        to = slice(DH * part, DH * (part + 1))
                        sp.dma_start(f(q_stack[g][to, i, :]), f(q_part[g][r, :])).then_inc(stacked[g].sem, 16)
                        sp.dma_start(f(k_stack[g][to, i, :]), f(k_part[g][r, :])).then_inc(stacked[g].sem, 16)

            def place_max(j, t):
                g, i = j // GH, j % GH
                sp.wait_ge(dve_done.sem, dve_done.after(f"m{j}", t))
                sp.nop(nofuse=True)
                sp.dma_start(f(q_stack[g][STACK:STACK + 1, i, :]), f(neg_max[:, j % 2, :])).then_inc(max_placed[i].sem, 16)

            def iteration(t, par):
                if on(t, 1):
                    sp.wait_ge(dve_done.sem, dve_done.after("l_max3", t - 1))
                    sp.nop(nofuse=True)
                    sp.dma_start(adj_in[:, :, :], rows(adj, t + 1)).then_inc(adj_loaded.sem, 16)
                if on(t, 0):
                    sp.wait_ge(st_done.sem, st_done.after(POS - 1, t - 1))
                    sp.nop(nofuse=True)
                    stack(1, t)
                    place_max(4, t)
                    place_max(5, t)
                if on(t, -1):
                    sp.wait_ge(pool_done.sem, pool_done.after("diag", t))
                    sp.nop(nofuse=True)
                    sp.wait_ge(dve_done.sem, dve_done.after("l_max3", t - 1))
                    sp.nop(nofuse=True)
                    sp.dma_start(adj_in[:, :, :], rows(adj, t - 1)).then_inc(adj_loaded.sem, 16)
                if on(t, 0):
                    place_max(6, t)
                for half in range(2):
                    if on(t, -2):
                        sp.wait_ge(dve_done.sem, dve_done.after(f"fin{half}", t))
                        sp.nop(nofuse=True)
                        c = 2 * half
                        sp.dma_start(rows(out, t - 2, c, c + 2), h[par][:, c:c + 2, :]).then_inc(stored[half].sem, 16)
                if on(t, 0):
                    place_max(7, t)
                if on(t, 1):
                    sp.wait_ge(st_done.sem, st_done.after(POS // 2 - 1, t))
                    sp.nop(nofuse=True)
                    stack(0, t)
                    place_max(0, t)
                if on(t, 0):
                    for half in range(2):
                        sp.wait_ge(stored[half].sem, stored[half].after("out", t))
                        sp.nop(nofuse=True)
                    sp.dma_start(h[par][:, :, :], rows(x, t)).then_inc(h_loaded.sem, 16)
                if on(t, 1):
                    place_max(1, t)
                    place_max(2, t)
                if on(t, 2):
                    sp.wait_ge(pe_done.sem, pe_done.after("xt1", t))
                    sp.nop(nofuse=True)
                    sp.wait_ge(dve_done.sem, dve_done.after("o_lo0", t))
                    sp.nop(nofuse=True)
                    sp.dma_start(x_in[:, :, :], rows(x, t + 2)).then_inc(x_loaded.sem, 16)
                if on(t, 1):
                    place_max(3, t)

            sp.wait_ge(setup_pe, 6)
            program(sp, iteration)
            for half in range(2):
                sp.wait_ge(stored[half].sem, stored[half].after("out", LAST))
                sp.nop(nofuse=True)

        @block.tensor
        def _(pe):
            N_CONST = 17
            pe.wait_ge(ident_made, 9)
            pe.wait_ge(const_loaded, 16 * N_CONST)
            setup_banks = [*shared, *sm_bank, o_bank]
            for k in range(5):
                for i in range(DT):
                    for o in range(DT):
                        src = z[:, k, o * D + i * P:o * D + (i + 1) * P] if k < 4 else h[0][:, o, i * P:(i + 1) * P]
                        last = nc.tensor.transpose(setup_banks[k][:, (i * DT + o) * P:(i * DT + o + 1) * P],
                                                   src, ident[:, :])
                last.then_inc(setup_pe, 1)
            pe.wait_ge(setup_dve, 1)
            for i in range(DT):
                for o in range(DT):
                    last = nc.tensor.matmul(setup_banks[5][:, i * P:(i + 1) * P], h[0][:, o, i * P:(i + 1) * P],
                                            zt[:, 0, o * P:(o + 1) * P], start=(o == 0), stop=(o == DT - 1))
            last.then_inc(setup_pe, 1)
            pe.wait_ge(setup_dve, 8)

            def bank_read(name, t):
                other, tb = name, t
                while True:
                    other, earlier = before[other]
                    tb = tb - 1 if earlier else tb
                    if on(tb, OFF[other]) or tb < FIRST:
                        break
                who, reader = READ_BY[other]
                return made[who].sem, made[who].after(reader, tb)

            def three_terms(bank, terms, kts=DT):
                for kt in range(kts):
                    (ah, al), (bh, bl) = terms(kt)
                    for n, (a, b) in enumerate(((ah, bh), (ah, bl), (al, bh))):
                        last = nc.tensor.matmul(bank, a, b, start=(kt == 0 and n == 0), stop=(kt == kts - 1 and n == 2))
                return last

            def iteration(t, par):
                nxt = 1 - par

                def turn_x(kt):
                    if kt == 0:
                        pe.wait_ge(x_loaded.sem, x_loaded.after("x", t - 1))
                    pe.wait_ge(*bank_read(f"xt{kt}", t))
                    bank = bank_of[f"xt{kt}"]
                    for c in range(NT):
                        last = nc.tensor.transpose(bank[:, c * P:(c + 1) * P], x_in[:, c, kt * P:(kt + 1) * P], ident[:, :])
                    last.then_inc(pe_done.sem, 1)

                def project_qk(name, w, g):
                    pe.wait_ge(dve_done.sem, dve_done.after("x_lo1", t))
                    pe.wait_ge(*bank_read(f"{name}{g}", t))
                    bank = bank_of[f"{name}{g}"]
                    o = slice(g * P, (g + 1) * P)
                    three_terms(bank[:, :], lambda kt: ((weight_hi[:, w, kt, o], weight_lo[:, w, kt, o]),
                                                        (xt_hi[:, kt, :], xt_lo[:, kt, :]))).then_inc(pe_done.sem, 1)

                def rows_times(name, half, hi, lo, w):
                    pe.wait_ge(*bank_read(f"{name}{half}", t))
                    bank = bank_of[f"{name}{half}"]
                    for k in range(2):
                        n = slice((2 * half + k) * P, (2 * half + k + 1) * P)
                        last = three_terms(bank[:, k * D:(k + 1) * D],
                                           lambda kt: ((hi[:, kt, n], lo[:, kt, n]),
                                                       (weight_hi[:, w, kt, :], weight_lo[:, w, kt, :])))
                    last.then_inc(pe_done.sem, 1)

                def out_project(half):
                    if half == 0:
                        pe.wait_ge(dve_done.sem, dve_done.after("o_lo1", t))
                    rows_times("op", half, o_hi, o_lo, WO)

                def fc_project(half):
                    if half == 0:
                        pe.wait_ge(dve_done.sem, dve_done.after("h_lo1", t))
                    rows_times("fc", half, ht_hi, ht_lo, FC)

                def turn_mask(half):
                    if half == 0:
                        pe.wait_ge(pool_done.sem, pool_done.after("diag", t))
                    pe.wait_ge(*bank_read(f"mt{half}", t))
                    bank = bank_of[f"mt{half}"][:, :].bitcast(BF16)
                    for k in range(2):
                        for c in range(NT):
                            key = (2 * half + k) * P
                            last = nc.tensor.transpose(bank[:, k * N + c * P:k * N + (c + 1) * P],
                                                       mask[nxt][:, c * N + key:c * N + key + P], ident_b[:, :])
                    last.then_inc(pe_done.sem, 1)

                def turn_max(j):
                    pe.wait_ge(max_done.sem, max_done.after((4 * j + 15) % POS, t if j < 4 else t - (1 if 4 * j + 15 < POS else 0)))
                    pe.wait_ge(*bank_read(f"m{j}", t))
                    bank = bank_of[f"m{j}"]
                    nc.tensor.transpose(bank[0:NT, 0:P], row_max[:, j, :], ident[:, :]).then_inc(pe_done.sem, 1)

                def times_v(k):
                    kt = (k - 1) % NT
                    g, vv = (1, v[nxt]) if k == 0 else ((k - 1) // NT, v[par])
                    pe.wait_ge(exp_done.sem, exp_done.after((4 * k - 1) % POS, t if k else t - 1))
                    if k == 1:
                        pe.wait_ge(act_done.sem, act_done.after("v1", t - 1))
                    if kt == 0:
                        pe.wait_ge(act_done.sem, act_done.after(f"o_raw{1 - g}", t))
                    for i in range(GH):
                        o = g * P + i * DH
                        last = nc.tensor.matmul(o_bank[i * DH:(i + 1) * DH, :], vv[:, kt, o:o + DH], e[:, kt, i, :],
                                                start=(kt == 0), stop=(kt == NT - 1))
                    last.then_inc(pe_done.sem, 1)

                def total(g):
                    pe.wait_ge(pool_done.sem, pool_done.after(f"sum{g}_3", t))
                    pe.wait_ge(*bank_read(f"sum{g}", t))
                    bank = bank_of[f"sum{g}"]
                    for i in range(GH):
                        last = nc.tensor.matmul(bank[i * DH:(i + 1) * DH, :], ones[:, :], e_sum[:, i, :], start=True, stop=True)
                    last.then_inc(pe_done.sem, 1)

                def turn_h(kt):
                    if kt == 0:
                        pe.wait_ge(dve_done.sem, dve_done.after("h_b", t))
                    pe.wait_ge(*bank_read(f"ht{kt}", t))
                    bank = bank_of[f"ht{kt}"]
                    for c in range(NT):
                        last = nc.tensor.transpose(bank[:, c * P:(c + 1) * P], h[nxt][:, c, kt * P:(kt + 1) * P], ident[:, :])
                    last.then_inc(pe_done.sem, 1)

                def key_logits():
                    pe.wait_ge(*bank_read("kb", t))
                    bank = bank_of["kb"]
                    three_terms(bank[:, :], lambda kt: ((uk_hi[:, kt, :], uk_lo[:, kt, :]),
                                                        (ht_hi[:, kt, :], ht_lo[:, kt, :]))).then_inc(pe_done.sem, 1)

                def turn_z(c):
                    pe.wait_ge(act_done.sem, act_done.after(f"lexp{c}", t))
                    pe.wait_ge(*bank_read(f"et{c}", t))
                    bank = bank_of[f"et{c}"]
                    for k in range(NT):
                        last = nc.tensor.transpose(bank[:, k * P:(k + 1) * P], z[:, c, k * P:(k + 1) * P], ident[:, :])
                    last.then_inc(pe_done.sem, 1)

                def attend(c):
                    half, k = c // 2, c % 2
                    if c == 0:
                        pe.wait_ge(act_done.sem, act_done.after("et3", t))
                    if k == 0:
                        pe.wait_ge(*bank_read(f"at{half}", t))
                    bank = bank_of[f"at{half}"]
                    for kt in range(NT):
                        last = nc.tensor.matmul(bank[:, k * D:(k + 1) * D], zt[:, kt, c * P:(c + 1) * P], feat[:, kt, :],
                                                start=(kt == 0), stop=(kt == NT - 1))
                    if k == 1:
                        last.then_inc(pe_done.sem, 1)

                for s in range(POS):
                    g, kt, i = s // (POS // 2), s // GH % NT, s % GH
                    if on(t, 0):
                        if kt == 0 and i == 0:
                            pe.wait_ge(stacked[g].sem, stacked[g].after(f"g{g}", t if g else t - 1))
                            if g == 0:
                                pe.wait_ge(act_done.sem, act_done.after("mt1", t - 1))
                        if kt == 0:
                            pe.wait_ge(max_placed[i].sem, max_placed[i].after(f"g{g}", t if g else t - 1))
                        pe.wait_ge(exp_done.sem, exp_done.after((s - 2) % POS, t if s >= 2 else t - 1))
                        bank = st_bank[s % 2]
                        nc.tensor.matmul(bank[:, :], k_stack[g][:, i, kt * P:(kt + 1) * P], q_stack[g][:, i, :],
                                         start=True, stop=False)
                        nc.tensor.matmul(bank[:, :], ident_b[:, :], mask_t[par][:, kt, :],
                                         start=False, stop=True).then_inc(st_done.sem, 1)
                    off, j, qt = maxima_tile(s)
                    if on(t, off):
                        if j % GH == 0 and qt == 0:
                            pe.wait_ge(act_done.sem, act_done.after(f"k_hi{j // GH}", t))
                        pe.wait_ge(max_done.sem, max_done.after((s - 2) % POS, t if s >= 2 else t - 1))
                        r = slice(DH * (j % GH), DH * (j % GH + 1))
                        nc.tensor.matmul(sm_bank[s % 2][:, :], qt_hi[j // GH][r, qt * P:(qt + 1) * P],
                                         kt_hi[j // GH][r, :], start=True, stop=True).then_inc(sm_done.sem, 1)
                    if s == 0:
                        if on(t, 1):
                            turn_x(0)
                    if s == 1:
                        if on(t, 1):
                            turn_x(1)
                        if on(t, 0):
                            turn_max(4)
                    if s == 2:
                        if on(t, -1):
                            times_v(0)
                    if s == 3:
                        if on(t, 1):
                            project_qk("q", WQ, 0)
                    if s == 4:
                        if on(t, 1):
                            project_qk("k", WK, 0)
                        if on(t, -2):
                            turn_z(0)
                    if s == 5:
                        if on(t, 0):
                            turn_max(5)
                    if s == 6:
                        if on(t, 0):
                            times_v(1)
                        if on(t, -2):
                            turn_z(1)
                        if on(t, -1):
                            total(1)
                    if s == 7:
                        if on(t, -2):
                            turn_z(2)
                    if s == 8:
                        if on(t, -2):
                            turn_z(3)
                    if s == 9:
                        if on(t, 0):
                            turn_max(6)
                        if on(t, -2):
                            attend(0)
                    if s == 10:
                        if on(t, 0):
                            times_v(2)
                        if on(t, -2):
                            attend(1)
                    if s == 11:
                        if on(t, -2):
                            attend(2)
                    if s == 12:
                        if on(t, -2):
                            attend(3)
                    if s == 13:
                        if on(t, 0):
                            turn_max(7)
                        if on(t, -1):
                            out_project(0)
                    if s == 14:
                        if on(t, 0):
                            times_v(3)
                        if on(t, -1):
                            out_project(1)
                    if s == 15:
                        if on(t, 1):
                            turn_mask(0)
                    if s == 16:
                        if on(t, 1):
                            turn_mask(1)
                    if s == 17:
                        if on(t, 1):
                            turn_max(0)
                            project_qk("q", WQ, 1)
                    if s == 18:
                        if on(t, 0):
                            times_v(4)
                        if on(t, 1):
                            project_qk("k", WK, 1)
                    if s == 19:
                        if on(t, 1):
                            rows_times("v", 0, xt_hi, xt_lo, WV)
                    if s == 20:
                        if on(t, 1):
                            rows_times("v", 1, xt_hi, xt_lo, WV)
                    if s == 21:
                        if on(t, 1):
                            turn_max(1)
                    if s == 22:
                        if on(t, 0):
                            times_v(5)
                        if on(t, -1):
                            turn_h(0)
                        if on(t, 0):
                            total(0)
                    if s == 23:
                        if on(t, -1):
                            turn_h(1)
                    if s == 25:
                        if on(t, 1):
                            turn_max(2)
                    if s == 26:
                        if on(t, 0):
                            times_v(6)
                        if on(t, -1):
                            fc_project(0)
                    if s == 27:
                        if on(t, -1):
                            fc_project(1)
                    if s == 28:
                        if on(t, -1):
                            key_logits()
                    if s == 29:
                        if on(t, 1):
                            turn_max(3)
                    if s == 30:
                        if on(t, 0):
                            times_v(7)

            program(pe, iteration)

        @block.scalar
        def _(act):
            for k in range(5):
                act.wait_ge(setup_pe, k + 1)
                bank = [*shared, *sm_bank][k]
                nc.scalar.copy(weight_hi[:, k, :, :], bank[:, :].rearrange("p (i o) -> p i o", i=DT)).then_inc(setup_act, 1)
            act.wait_ge(setup_pe, 6)
            nc.scalar.copy(uk_hi[:, :, :], o_bank[:, 0:DT * P].rearrange("p (i o) -> p i o", i=DT)).then_inc(setup_act, 1)
            act.wait_ge(const_loaded, 16 * 17)

            def iteration(t, par):
                nxt = 1 - par

                def logits(c, tb):
                    act.wait_ge(dve_done.sem, dve_done.after("l_max3", tb))
                    nc.scalar.activation(z[:, c, :], z[:, c, :], ACT.Identity, bias=q_bias[:, c:c + 1])\
                        .then_inc(act_done.sem, 1)

                def exponentials(c):
                    act.wait_ge(dve_done.sem, dve_done.after(f"leaky{c}", t))
                    nc.scalar.activation(z[:, c, :], z[:, c, :], ACT.Exp, bias=l_negmax[:, c:c + 1],
                                         accum_out=l_sum[:, c:c + 1]).then_inc(act_done.sem, 1)

                def copy(dst, name, bank_ap):
                    act.wait_ge(pe_done.sem, pe_done.after(name, t))
                    nc.scalar.copy(dst, bank_ap).then_inc(act_done.sem, 1)

                for s in range(POS):
                    g, kt, i = s // (POS // 2), s // GH % NT, s % GH
                    if on(t, 0):
                        act.wait_ge(st_done.sem, st_done.after(s, t))
                        if i == 0:
                            n = max(kt, 1)
                            if g == 1:
                                act.wait_ge(pe_done.sem, pe_done.after(f"pv{kt + 1}", t))
                                act.wait_ge(pool_done.sem, pool_done.after(f"sum0_{n}", t))
                            elif kt < NT - 1:
                                act.wait_ge(pe_done.sem, pe_done.after(f"pv{kt + 5}", t - 1))
                                act.wait_ge(pool_done.sem, pool_done.after(f"sum1_{n}", t - 1))
                            else:
                                act.wait_ge(pe_done.sem, pe_done.after("pv0", t))
                                act.wait_ge(pool_done.sem, pool_done.after("sum1_3", t))
                        nc.scalar.activation(e[:, kt, i, :], st_bank[s % 2][:, :], ACT.Exp, scale=SCALE)\
                            .then_inc(exp_done.sem, 1)
                    if s == 0 and on(t, -2):
                        logits(2, t - 1)
                        logits(3, t - 1)
                    if s in (1, 2) and on(t, 1):
                        copy(xt_hi[:, s - 1, :], f"xt{s - 1}", bank_of[f"xt{s - 1}"][:, :])
                    if s in (1, 2) and on(t, -2):
                        exponentials(s - 1)
                    if s == 3 and on(t, -1):
                        copy(o_raw, "pv0", o_bank[:, :])
                    if s in (4, 5, 18, 19) and on(t, 1):
                        g2 = 0 if s < 6 else 1
                        name, dst, k = (("q", qt_hi, 0), ("k", kt_hi, 1))[(s - 4) % 14]
                        act.wait_ge(pe_done.sem, pe_done.after(f"{name}{g2}", t))
                        act.wait_ge(stacked[g2].sem, stacked[g2].after(f"g{g2}", t - 1 if g2 == 0 else t))
                        nc.scalar.activation(dst[g2][:, :], bank_of[f"{name}{g2}"][:, :], ACT.Identity,
                                             bias=bias_col[:, k, g2:g2 + 1]).then_inc(act_done.sem, 1)
                    if s in (5, 7, 8, 9) and on(t, -2):
                        c = (5, 7, 8, 9).index(s)
                        copy(zt[:, :, c * P:(c + 1) * P], f"et{c}",
                             bank_of[f"et{c}"][:, :].rearrange("p (k n) -> p k n", k=NT))
                    if s in (5, 6) and on(t, -2):
                        exponentials(s - 3)
                    if s == 19 and on(t, 0):
                        copy(o_raw, "pv4", o_bank[:, :])
                    if s in (10, 26) and on(t, -1 if s == 10 else 0):
                        g2 = 1 if s == 10 else 0
                        act.wait_ge(dve_done.sem, dve_done.after(f"o_norm{g2}", t))
                        nc.scalar.activation(o_hi[:, g2, :], o_raw, ACT.Identity,
                                             bias=bias_col[:, 2, g2:g2 + 1]).then_inc(act_done.sem, 1)
                    if s in (16, 17) and on(t, 1):
                        half = s - 16
                        copy(mask_t[nxt][:, 2 * half:2 * half + 2, :], f"mt{half}",
                             bank_of[f"mt{half}"][:, :].bitcast(BF16).rearrange("p (k n) -> p k n", k=2))
                    if s in (20, 21) and on(t, 1):
                        half = s - 20
                        copy(v[nxt][:, 2 * half:2 * half + 2, :], f"v{half}",
                             bank_of[f"v{half}"][:, :].rearrange("p (k n) -> p k n", k=2))
                    if s in (23, 24) and on(t, -1):
                        copy(ht_hi[:, s - 23, :], f"ht{s - 23}", bank_of[f"ht{s - 23}"][:, :])
                    if s in (27, 28) and on(t, -1):
                        half = s - 27
                        copy(feat[:, 2 * half:2 * half + 2, :], f"fc{half}",
                             bank_of[f"fc{half}"][:, :].rearrange("p (k n) -> p k n", k=2))
                    if s == POS - 1 and on(t, -1):
                        logits(0, t)
                        logits(1, t)

            program(act, iteration)

        @block.vector
        def _(dve):
            dve.wait_ge(const_loaded, 16 * 17)
            dve.wait_ge(ident_made, 9)
            for o in range(DT):
                last = nc.vector.tensor_scalar(zt[:, 0, o * P:(o + 1) * P], zt[:, 1, 0:P], kw_col[:, o:o + 1], None, ALU.add)
            last.then_inc(setup_dve, 1)
            for k, row in enumerate((qw_row[:, :], zt[:, 2, 0:D])):
                last = nc.vector.tensor_tensor_reduce(zt[:, 3, k * D:(k + 1) * D], fcb_row[:, :], row, 1.0, 0.0, ALU.mult, ALU.add,
                                                      logit_bias[:, k:k + 1])
            for k in range(6):
                dve.wait_ge(setup_act, k + 1)
                hi, lo = (weight_hi[:, k, :, :], weight_lo[:, k, :, :]) if k < 5 else (uk_hi[:, :, :], uk_lo[:, :, :])
                bank = [*shared, *sm_bank, o_bank][k][:, 0:512 if k < 5 else DT * P]
                nc.vector.tensor_tensor(lo, bank.rearrange("p (i o) -> p i o", i=DT), f(hi), ALU.subtract).then_inc(setup_dve, 1)
            dve.wait_ge(setup_dve, 7)
            nc.vector.tensor_tensor(logit_bias[:, 0:2], logit_bias[:, 0:2], qkb[:, :], ALU.add).then_inc(setup_dve, 1)
            dve.wait_ge(setup_dve, 8)
            nc.vector.tensor_tensor(logit_bias[:, 3:4], logit_bias[:, 0:1], logit_bias[:, 1:2], ALU.add).then_inc(setup_dve, 1)
            dve.wait_ge(setup_dve, 9)

            def iteration(t, par):
                nxt = 1 - par
                done = dve_done.sem

                def lo_part(dst, name, hi_ready, hi):
                    dve.wait_ge(act_done.sem, act_done.after(hi_ready, t))
                    nc.vector.tensor_tensor(dst, bank_of[name][:, :], f(hi), ALU.subtract).then_inc(done, 1)

                def qk_lo(name, g, k, dst, hi):
                    dve.wait_ge(act_done.sem, act_done.after(f"{name}_hi{g}", t))
                    nc.vector.scalar_tensor_tensor(dst[g][:, :], bank_of[f"{name}{g}"][:, :], bias_col[:, k, g:g + 1],
                                                   f(hi[g][:, :]), ALU.add, ALU.subtract).then_inc(done, 1)

                def negate_max(j):
                    dve.wait_ge(pe_done.sem, pe_done.after(f"m{j}", t))
                    i2, g2 = (j - 2) % GH, (j - 2) % NH // GH
                    tb = t - 1 if j in (4, 5) else t
                    dve.wait_ge(max_placed[i2].sem, max_placed[i2].after(f"g{g2}", tb))
                    nc.vector.tensor_scalar(neg_max[:, j % 2, :], bank_of[f"m{j}"][0:NT, 0:P], -1.0, None, ALU.mult)\
                        .then_inc(done, 1)

                def reciprocals(g, half):
                    if half == 0:
                        dve.wait_ge(pe_done.sem, pe_done.after(f"sum{g}", t))
                    for k in range(2):
                        n = slice((2 * half + k) * P, (2 * half + k + 1) * P)
                        last = nc.vector.reciprocal(recip[:, n], bank_of[f"sum{g}"][:, n])
                    last.then_inc(done, 1)

                def normalise(g):
                    dve.wait_ge(act_done.sem, act_done.after(f"o_raw{g}", t))
                    dve.wait_ge(dve_done.sem, dve_done.after(f"recip{g}b", t))
                    nc.vector.tensor_tensor(o_raw, o_raw, recip, ALU.mult).then_inc(done, 1)

                def o_low(g):
                    dve.wait_ge(act_done.sem, act_done.after(f"o_hi{g}", t))
                    nc.vector.scalar_tensor_tensor(o_lo[:, g, :], o_raw, bias_col[:, 2, g:g + 1], f(o_hi[:, g, :]),
                                                   ALU.add, ALU.subtract).then_inc(done, 1)

                def finish(half):
                    dve.wait_ge(pe_done.sem, pe_done.after(f"at{half}", t))
                    if half == 0:
                        dve.wait_ge(dve_done.sem, dve_done.after("l_recip", t))
                    for k in range(2):
                        c = 2 * half + k
                        last = nc.vector.scalar_tensor_tensor(h[par][:, c, :], bank_of[f"at{half}"][:, k * D:(k + 1) * D],
                                                              l_recip[:, c:c + 1], h[par][:, c, :], ALU.mult, ALU.add)
                    last.then_inc(done, 1)

                def add_residual(half):
                    dve.wait_ge(pe_done.sem, pe_done.after(f"op{half}", t))
                    if half == 0:
                        dve.wait_ge(pool_done.sem, pool_done.after("x_bo", t))
                    hc = h[nxt][:, 2 * half:2 * half + 2, :]
                    nc.vector.tensor_tensor(hc, bank_of[f"op{half}"][:, :].rearrange("p (k n) -> p k n", k=2), hc, ALU.add)\
                        .then_inc(done, 1)

                def query_logits(half):
                    dve.wait_ge(act_done.sem, act_done.after(f"feat{half}", t))
                    if half == 0:
                        dve.wait_ge(pe_done.sem, pe_done.after("et3", t))
                    for k in range(2):
                        c = 2 * half + k
                        last = nc.vector.tensor_tensor_reduce(z[:, c, 0:D], feat[:, c, :], qw_row[:, :], 1.0, 0.0,
                                                              ALU.mult, ALU.add, q_dot[:, c:c + 1])
                    last.then_inc(done, 1)

                def leaky(c):
                    dve.wait_ge(act_done.sem, act_done.after(f"logit{c}", t if c > 1 else t - 1))
                    nc.vector.scalar_tensor_tensor(z[:, c, :], z[:, c, :], SLOPE, z[:, c, :], ALU.mult, ALU.max)\
                        .then_inc(done, 1)

                def layer1_maxima(half):
                    if half == 0:
                        dve.wait_ge(pe_done.sem, pe_done.after("kb", t))
                        dve.wait_ge(pool_done.sem, pool_done.after("l_mask", t))
                        dve.nop(nofuse=True)
                    for k in range(2):
                        c = 2 * half + k
                        last = nc.vector.tensor_tensor_reduce(z[:, c, :], bank_of["kb"][:, :], adj_in[:, c, :], 1.0, LOWEST,
                                                              ALU.add, ALU.max, l_max[:, c:c + 1])
                    last.then_inc(done, 1)

                for s in range(POS):
                    off, j, qt = maxima_tile(s)
                    if on(t, off):
                        if off == 1 and j == 0 and qt == 0:
                            dve.wait_ge(pool_done.sem, pool_done.after("diag", t))
                        dve.wait_ge(sm_done.sem, sm_done.after(s, t))
                        dve.nop(nofuse=True)
                        nc.vector.tensor_tensor_reduce(sm_bank[s % 2][:, :], sm_bank[s % 2][:, :],
                                                       mask[nxt if off else par][:, qt * N:(qt + 1) * N], 1.0, LOWEST,
                                                       ALU.add, ALU.max, row_max[:, j, qt:qt + 1]).then_inc(max_done.sem, 1)
                    if s == 0 and on(t, -2):
                        leaky(0)
                        leaky(1)
                    if s in (1, 2) and on(t, 1):
                        lo_part(xt_lo[:, s - 1, :], f"xt{s - 1}", f"x_hi{s - 1}", xt_hi[:, s - 1, :])
                    if s == 1 and on(t, -2):
                        leaky(2)
                    if s == 2 and on(t, 0):
                        negate_max(4)
                    if s == 2 and on(t, -2):
                        leaky(3)
                    if s == 4 and on(t, 1):
                        qk_lo("q", 0, 0, qt_lo, qt_hi)
                    if s == 5 and on(t, 1):
                        qk_lo("k", 0, 1, kt_lo, kt_hi)
                    if s == 6 and on(t, 1):
                        dve.wait_ge(adj_loaded.sem, adj_loaded.after("adj", t))
                        nc.vector.tensor_scalar(mask[nxt], adj_in[:, :, :].rearrange("p c n -> p (c n)"),
                                                0.0, -BIG, ALU.is_le, ALU.mult).then_inc(done, 1)
                    if s == 6 and on(t, 0):
                        negate_max(5)
                    if s in (7, 8) and on(t, -1):
                        reciprocals(1, s - 7)
                    if s == 9 and on(t, -1):
                        normalise(1)
                    if s == 10 and on(t, 0):
                        negate_max(6)
                    if s == 11 and on(t, -2):
                        dve.wait_ge(act_done.sem, act_done.after("lexp3", t))
                        nc.vector.reciprocal(l_recip[:, :], l_sum[:, :]).then_inc(done, 1)
                        dve.wait_ge(pool_done.sem, pool_done.after("h_fcb", t - 1))
                        finish(0)
                    if s == 11 and on(t, -1):
                        o_low(1)
                    if s == 13 and on(t, -2):
                        finish(1)
                    if s == 14 and on(t, 0):
                        negate_max(7)
                    if s == 14 and on(t, -1):
                        add_residual(0)
                    if s == 15 and on(t, -1):
                        add_residual(1)
                        dve.wait_ge(dve_done.sem, dve_done.after("h_add1", t))
                        for c in range(NT):
                            last = nc.vector.bn_stats(stats[:, c, :], h[nxt][:, c, :])
                        last.then_inc(done, 1)
                    if s == 16 and on(t, -1):
                        dve.wait_ge(dve_done.sem, dve_done.after("stats", t))
                        dve.nop(nofuse=True)
                        for c in range(NT):
                            last = nc.vector.bn_aggr(moments[:, c, :], stats[:, c, :])
                        last.then_inc(done, 1)
                        dve.wait_ge(dve_done.sem, dve_done.after("moments", t))
                        nc.vector.tensor_scalar(var_eps[:, :], moments[:, :, 1], EPS, None, ALU.add).then_inc(done, 1)
                    if s == 17 and on(t, -1):
                        for c in range(NT):
                            last = nc.vector.scalar_tensor_tensor(h[nxt][:, c, :], h[nxt][:, c, :], moments[:, c, 0:1],
                                                                  gamma_row[:, :], ALU.subtract, ALU.mult)
                        last.then_inc(done, 1)
                    if s == 18 and on(t, 1):
                        negate_max(0)
                        qk_lo("q", 1, 0, qt_lo, qt_hi)
                    if s == 19 and on(t, 1):
                        qk_lo("k", 1, 1, kt_lo, kt_hi)
                    if s in (19, 20) and on(t, -1):
                        if s == 19:
                            dve.wait_ge(pool_done.sem, pool_done.after("rstd", t))
                            dve.wait_ge(dve_done.sem, dve_done.after("centre", t))
                        for c in range(2 * (s - 19), 2 * (s - 19) + 2):
                            last = nc.vector.scalar_tensor_tensor(h[nxt][:, c, :], h[nxt][:, c, :], rstd[:, c:c + 1],
                                                                  beta_row[:, :], ALU.mult, ALU.add)
                        last.then_inc(done, 1)
                    if s == 22 and on(t, 1):
                        negate_max(1)
                    if s in (23, 24) and on(t, 0):
                        reciprocals(0, s - 23)
                    if s in (24, 25) and on(t, -1):
                        lo_part(ht_lo[:, s - 24, :], f"ht{s - 24}", f"h_hi{s - 24}", ht_hi[:, s - 24, :])
                    if s == 25 and on(t, 0):
                        normalise(0)
                    if s == 26 and on(t, 1):
                        negate_max(2)
                    if s == 27 and on(t, -1):
                        query_logits(0)
                    if s == 27 and on(t, 0):
                        o_low(0)
                    if s == 28 and on(t, -1):
                        query_logits(1)
                        dve.wait_ge(dve_done.sem, dve_done.after("q_dot1", t))
                        nc.vector.tensor_scalar(q_bias[:, :], q_dot[:, :], logit_bias[:, 3:4], None, ALU.add).then_inc(done, 1)
                    if s == 29 and on(t, -1):
                        layer1_maxima(0)
                    if s == 30 and on(t, 1):
                        negate_max(3)
                    if s == 30 and on(t, -1):
                        layer1_maxima(1)
                        dve.wait_ge(dve_done.sem, dve_done.after("l_max3", t))
                        nc.vector.tensor_tensor(l_z[:, :], l_max[:, :], q_bias[:, :], ALU.add).then_inc(done, 1)
                        dve.wait_ge(dve_done.sem, dve_done.after("l_z", t))
                        nc.vector.tensor_scalar(l_nz[:, :], l_z[:, :], -1.0, None, ALU.mult).then_inc(done, 1)
                        dve.wait_ge(dve_done.sem, dve_done.after("l_nz", t))
                        nc.vector.scalar_tensor_tensor(l_negmax[:, :], l_nz[:, :], SLOPE, l_nz[:, :], ALU.mult, ALU.min)\
                            .then_inc(done, 1)

            program(dve, iteration)

        @block.gpsimd
        def _(pool):
            for ap in (ident, ident_b):
                nc.gpsimd.memset(ap[:, :], 0.0).then_inc(ident_made, 1)
            pool.wait_ge(ident_made, 2)
            for ap in (ident, ident_b):
                nc.gpsimd.affine_select(out=ap[:, :], in_=ap[:, :], compare_op=ALU.not_equal, fill=1.0, base=0,
                                        pattern=[[-1, P]], channel_multiplier=1).then_inc(ident_made, 1)
            for n, (ap, value) in enumerate((*((f(k_stack[g][STACK:STACK + 1, :, :]), 1.0) for g in range(NG)),
                                             (minus_half[:, :], -0.5), (zt[:, 1, 0:P], 0.0), (ones[:, :], 1.0))):
                pool.wait_ge(ident_made, 4 + n)
                nc.gpsimd.memset(ap, value).then_inc(ident_made, 1)
            pool.wait_ge(const_loaded, 16 * 17)

            def iteration(t, par):
                nxt = 1 - par

                def add_e(g, n):
                    slot = (g * NT + n) * GH + GH - 1
                    tb = t if (g, n) != (1, 3) else t - 1
                    pool.wait_ge(exp_done.sem, exp_done.after(slot, tb))
                    if n == 1:
                        pool.wait_ge(pe_done.sem, pe_done.after(f"sum{1 - g}", t))
                        a, b = e[:, 0, :, :], e[:, 1, :, :]
                    else:
                        pool.wait_ge(pool_done.sem, pool_done.after(f"sum{g}_{n - 1}", tb))
                        a, b = e_sum[:, :, :], e[:, n, :, :]
                    nc.gpsimd.tensor_tensor(e_sum[:, :, :], a, b, ALU.add).then_inc(pool_done.sem, 1)

                if on(t, -1):
                    add_e(1, 3)
                    pool.wait_ge(h_loaded.sem, h_loaded.after("x_again", t - 1))
                    hh = h[nxt]
                    nc.gpsimd.tensor_tensor(hh[:, :, :], hh[:, :, :], bo_row[:, :].unsqueeze(1).broadcast_to([P, NT, D]),
                                            ALU.add).then_inc(pool_done.sem, 1)
                if on(t, 1):
                    pool.wait_ge(dve_done.sem, dve_done.after("mask", t))
                    pool.nop(nofuse=True)
                    nc.gpsimd.affine_select(out=mask_diag[nxt], in_=mask_diag[nxt], compare_op=ALU.not_equal, fill=0.0, base=0,
                                            pattern=[[0, NT], [-1, P]], channel_multiplier=1).then_inc(pool_done.sem, 1)
                if on(t, 0):
                    add_e(0, 1)
                    add_e(0, 2)
                if on(t, -1):
                    pool.wait_ge(dve_done.sem, dve_done.after("var_eps", t))
                    nc.gpsimd.tensor_tensor(rstd[:, :], var_eps[:, :], minus_half[:, :], ALU.pow).then_inc(pool_done.sem, 1)
                if on(t, 0):
                    add_e(0, 3)
                if on(t, -1):
                    pool.wait_ge(adj_loaded.sem, adj_loaded.after("adj_again", t))
                    pool.nop(nofuse=True)
                    nc.gpsimd.tensor_scalar(adj_in[:, :, :], adj_in[:, :, :], -1.0, -NEG_INF, ALU.add, ALU.mult)\
                        .then_inc(pool_done.sem, 1)
                if on(t, 0):
                    add_e(1, 1)
                if on(t, -1):
                    pool.wait_ge(pe_done.sem, pe_done.after("ht1", t))
                    hh = h[nxt]
                    nc.gpsimd.tensor_tensor(hh[:, :, :], hh[:, :, :], fcb_row[:, :].unsqueeze(1).broadcast_to([P, NT, D]),
                                            ALU.add).then_inc(pool_done.sem, 1)
                if on(t, 0):
                    add_e(1, 2)

            program(pool, iteration)


_INS = ["x", "adj", "L0_gnn_Wq", "L0_gnn_bq", "L0_gnn_Wk", "L0_gnn_bk", "L0_gnn_Wv", "L0_gnn_bv", "L0_gnn_Wo",
        "L0_gnn_bo", "L0_gnn_gamma", "L0_gnn_beta", "L1_gnn_fc_w", "L1_gnn_fc_b", "L1_gnn_q_w", "L1_gnn_q_b",
        "L1_gnn_k_w", "L1_gnn_k_b"]


def kernel(**inputs):
    import numpy as _np
    import concourse.bacc as _bacc
    from concourse import mybir as _mybir
    from concourse.bass_utils import run_bass_kernel_spmd as _run

    nc = _bacc.Bacc("TRN2", target_bir_lowering=False, num_devices=1)
    arrays, args = {}, []
    for name in _INS:
        a = _np.ascontiguousarray(inputs[name])
        arrays[f"in_{name}"] = a
        args.append(nc.dram_tensor(f"in_{name}", a.shape, _mybir.dt.from_np(a.dtype), kind="ExternalInput").ap())
    args.append(nc.dram_tensor("out_y", (NB, N, D), F32, kind="ExternalOutput").ap())
    build(nc, *args)
    r = _run(nc, [arrays], core_ids=[0])
    return r.results[0]["out_y"]
```

```python
from contextlib import ExitStack

import concourse.bass as bass
from concourse import mybir

F32 = mybir.dt.float32
F32R = mybir.dt.float32r
BF16 = mybir.dt.bfloat16
ALU = mybir.AluOpType
ACT = mybir.ActivationFunctionType
AX = mybir.AxisListType

P = 128
NB, N, D = 16, 512, 256
NH, DH = 8, 32
GH = P // DH
NG = NH // GH
NT = N // P
DT = D // P
POS = NG * NT * GH
SCALE = float(DH) ** -0.5
BIG = 2.0 ** 100
NEG_INF = -1e9
SLOPE = 0.01
EPS = 1e-5
LOWEST = -3.0e38
STACK = 3 * DH
LEAD = 20

FIRST, LOOP_FROM, LOOP_TO, LAST = -1, 4, 14, NB + 1


def on(t, off):
    return not isinstance(t, int) or 0 <= t + off < NB


class Signal:

    def __init__(self, sem, steps, by=1):
        self.sem, self.by = sem, by
        self.place = {name: n for n, (name, _) in enumerate(steps)}
        self.offs = [off for _, off in steps]
        assert len(self.place) == len(steps)

    def after(self, step, t):
        last = self.place[step]
        if isinstance(t, int):
            return self.by * sum(min(max(t + off + (n <= last), 0), NB) for n, off in enumerate(self.offs))
        return t * (self.by * len(self.offs)) + self.by * sum(off + (n <= last) for n, off in enumerate(self.offs))


PE_STEPS = [
    (1, "xt0", 1), (2, "xt1", 1), (2, "m4", 0), (2, "pv0", -1), (3, "et0", -2), (4, "et1", -2), (4, "q0", 1),
    (5, "k0", 1), (6, "et2", -2), (6, "m5", 0), (6, "pv1", 0), (7, "et3", -2), (8, "sum1", -1),
    (10, "m6", 0), (10, "pv2", 0), (10, "at0", -2), (12, "at1", -2), (13, "op0", -1), (14, "m7", 0),
    (14, "pv3", 0), (15, "op1", -1), (16, "mt0", 1), (17, "mt1", 1), (18, "m0", 1), (18, "pv4", 0),
    (19, "q1", 1), (21, "k1", 1), (22, "m1", 1), (22, "pv5", 0), (22, "ht0", -1), (23, "ht1", -1),
    (24, "sum0", 0), (25, "fc0", -1), (26, "m2", 1), (26, "pv6", 0), (27, "fc1", -1), (28, "kb", -1),
    (29, "v0", 1), (30, "m3", 1), (30, "pv7", 0), (31, "v1", 1)]
OFF = {name: off for _, name, off in PE_STEPS}
FILLS = [name for _, name, _ in PE_STEPS if not name.startswith("pv")]
READ_BY = {
    "xt0": ("dve", "x_lo0"), "xt1": ("dve", "x_lo1"), "q0": ("dve", "q_lo0"), "k0": ("dve", "k_lo0"),
    "q1": ("dve", "q_lo1"), "k1": ("dve", "k_lo1"), "v0": ("act", "v0"), "v1": ("act", "v1"),
    "mt0": ("act", "mt0"), "mt1": ("act", "mt1"), "sum0": ("act", "sum0"), "sum1": ("act", "sum1"),
    "op0": ("dve", "h_add0"), "op1": ("dve", "h_add1"), "ht0": ("dve", "h_lo0"), "ht1": ("dve", "h_lo1"),
    "fc0": ("act", "feat0"), "fc1": ("act", "feat1"), "kb": ("dve", "l_max3"), "at0": ("dve", "fin0"),
    "at1": ("dve", "fin1"), **{f"et{c}": ("act", f"et{c}") for c in range(NT)},
    **{f"m{j}": ("dve", f"m{j}") for j in range(NH)}}
ACT_STEPS = [
    ("lexp0", -2), ("lexp1", -2), ("x_hi0", 1), ("lexp2", -2), ("x_hi1", 1), ("o_raw1", -1), ("lexp3", -2),
    ("et0", -2), ("q_hi0", 1), ("et1", -2), ("k_hi0", 1), ("et2", -2), ("et3", -2), ("sum1", -1), ("o_hi1", -1),
    ("mt0", 1), ("mt1", 1), ("o_raw0", 0), ("q_hi1", 1), ("k_hi1", 1), ("h_hi0", -1), ("h_hi1", -1), ("sum0", 0),
    ("feat0", -1), ("o_hi0", 0), ("feat1", -1), ("v0", 1), ("logit0", -1), ("logit1", -1), ("logit2", -1),
    ("logit3", -1), ("v1", 1)]
DVE_STEPS = [
    ("leaky1", -2), ("leaky2", -2), ("x_lo0", 1), ("leaky3", -2), ("x_lo1", 1), ("m4", 0),
    ("q_lo0", 1), ("k_lo0", 1), ("m5", 0), ("mask", 1), ("recip1", -1), ("m6", 0), ("o_norm1", -1), ("l_recip", -2),
    ("fin0", -2), ("o_lo1", -1), ("fin1", -2), ("h_add0", -1), ("m7", 0), ("h_add1", -1), ("stats", -1),
    ("moments", -1), ("var_eps", -1), ("centre", -1), ("m0", 1), ("q_lo1", 1), ("h_a", -1), ("h_b", -1), ("k_lo1", 1),
    ("m1", 1), ("h_lo0", -1), ("h_lo1", -1), ("recip0", 0), ("m2", 1), ("o_norm0", 0), ("q_dot0", -1),
    ("q_dot1", -1), ("q_bias", -1), ("o_lo0", 0), ("l_max1", -1), ("l_max3", -1), ("m3", 1), ("l_z", -1),
    ("l_nz", -1), ("l_negmax", -1), ("leaky0", -1)]
POOL_STEPS = [
    ("sum1_3", -1), ("x_bo", -1), ("diag", 1), ("sum0_1", 0), ("sum0_2", 0), ("rstd", -1), ("sum0_3", 0),
    ("l_mask", -1), ("sum1_1", 0), ("h_fcb", -1), ("sum1_2", 0)]


def maxima_tile(s):
    n = s - (POS - LEAD) if s >= POS - LEAD else s + LEAD
    return (1 if s >= POS - LEAD else 0), n // NT, n % NT


def build(nc, x, adj, wq, bq, wk, bk, wv, bv, wo, bo, gamma, beta, fc_w, fc_b, q_w, q_b, k_w, k_b, out):
    with ExitStack() as ctx:
        def sb(name, shape, dt=F32):
            return ctx.enter_context(nc.sbuf_tensor(name, shape, dt))

        def sem(name):
            return ctx.enter_context(nc.semaphore(name))

        weight_hi = sb("weight_hi", [P, 5, DT, D], F32R)
        weight_lo = sb("weight_lo", [P, 5, DT, D], F32R)
        WQ, WK, WV, WO, FC = range(5)
        uk_hi = sb("uk_hi", [P, DT, P], F32R)
        uk_lo = sb("uk_lo", [P, DT, P], F32R)
        bias_col = sb("bias_col", [P, 3, NG])
        gamma_row = sb("gamma_row", [P, D])
        beta_row = sb("beta_row", [P, D])
        bo_row = sb("bo_row", [P, D])
        fcb_row = sb("fcb_row", [P, D])
        qw_row = sb("qw_row", [P, D])
        kw_col = sb("kw_col", [P, DT])
        qkb = sb("qkb", [P, 2])
        logit_bias = sb("logit_bias", [P, 4])
        ident = sb("ident", [P, P])
        ident_b = sb("ident_b", [P, P], BF16)
        ones = sb("ones", [P, DH])
        minus_half = sb("minus_half", [P, NT])
        x_in = sb("x_in", [P, NT, D])
        adj_in = sb("adj_in", [P, NT, N])
        masks = sb("masks", [P, (2 * NT + 1) * N], BF16)
        mask = [masks[:, i * NT * N:(i + 1) * NT * N] for i in range(2)]
        mask_diag = [masks[:, i * NT * N:i * NT * N + NT * (N + P)].rearrange("p (c n) -> p c n", c=NT)[:, :, 0:P]
                     for i in range(2)]
        mask_t = [sb(f"mask_t{i}", [P, NT, N], BF16) for i in range(2)]
        xt_hi = sb("xt_hi", [P, DT, N], F32R)
        xt_lo = sb("xt_lo", [P, DT, N], F32R)
        qt_hi = [sb(f"qt_hi{g}", [P, N], F32R) for g in range(NG)]
        qt_lo = [sb(f"qt_lo{g}", [P, N], F32R) for g in range(NG)]
        kt_hi = [sb(f"kt_hi{g}", [P, N], F32R) for g in range(NG)]
        kt_lo = [sb(f"kt_lo{g}", [P, N], F32R) for g in range(NG)]
        q_stack = [sb(f"q_stack{g}", [STACK + 1, GH, N], F32R) for g in range(NG)]
        k_stack = [sb(f"k_stack{g}", [STACK + 1, GH, N], F32R) for g in range(NG)]
        v = [sb(f"v{i}", [P, NT, D]) for i in range(2)]
        row_max = sb("row_max", [P, NH, NT])
        neg_max = sb("neg_max", [NT, 2, P], F32R)
        e = sb("e", [P, NT, GH, N])
        e_sum = sb("e_sum", [P, GH, N])
        recip = x_in[:, 0:2, :].rearrange("p c d -> p (c d)")
        o_raw = x_in[:, 2:4, :].rearrange("p c d -> p (c d)")
        o_hi = sb("o_hi", [P, NG, N], F32R)
        o_lo = sb("o_lo", [P, NG, N], F32R)
        h = [sb(f"h{i}", [P, NT, D]) for i in range(2)]
        stats = sb("stats", [P, NT, 6])
        moments = sb("moments", [P, NT, 2])
        var_eps = sb("var_eps", [P, NT])
        rstd = sb("rstd", [P, NT])
        ht_hi = sb("ht_hi", [P, DT, N], F32R)
        ht_lo = sb("ht_lo", [P, DT, N], F32R)
        feat = sb("feat", [P, NT, D])
        z = sb("z", [P, NT, N])
        zt = sb("zt", [P, NT, N])
        q_dot = sb("q_dot", [P, NT])
        q_bias = sb("q_bias", [P, NT])
        l_max = sb("l_max", [P, NT])
        l_z = sb("l_z", [P, NT])
        l_nz = sb("l_nz", [P, NT])
        l_negmax = sb("l_negmax", [P, NT])
        l_sum = sb("l_sum", [P, NT])
        l_recip = sb("l_recip", [P, NT])

        def pb(name):
            return ctx.enter_context(nc.psum_tensor(name, [P, 512], F32))
        st_bank = [pb("st_bank0"), pb("st_bank1")]
        sm_bank = [pb("sm_bank0"), pb("sm_bank1")]
        o_bank = pb("o_bank")
        shared = [pb(f"shared{i}") for i in range(3)]
        bank_of = {name: shared[n % 3] for n, name in enumerate(FILLS)}
        before = {name: (FILLS[n - 3], n < 3) for n, name in enumerate(FILLS)}

        tiles = [(s, 0) for s in range(POS)]
        st_done = Signal(sem("st_done"), tiles)
        exp_done = Signal(sem("exp_done"), tiles)
        sm_tiles = [(s, maxima_tile(s)[0]) for s in range(POS)]
        sm_done = Signal(sem("sm_done"), sm_tiles)
        max_done = Signal(sem("max_done"), sm_tiles)
        pe_done = Signal(sem("pe_done"), [(name, off) for _, name, off in PE_STEPS])
        act_done = Signal(sem("act_done"), ACT_STEPS)
        dve_done = Signal(sem("dve_done"), DVE_STEPS)
        pool_done = Signal(sem("pool_done"), POOL_STEPS)
        made = {"act": act_done, "dve": dve_done}
        adj_loaded = Signal(sem("adj_loaded"), [("adj", 1), ("adj_again", -1)], 16)
        x_loaded = Signal(sem("x_loaded"), [("x", 2)], 16)
        h_loaded = Signal(sem("h_loaded"), [("x_again", 0)], 16)
        stacked = [Signal(sem("stacked0"), [("g0", 1)], 16 * 6 * GH), Signal(sem("stacked1"), [("g1", 0)], 16 * 6 * GH)]
        max_placed = [Signal(sem(f"max_placed{i}"), [("g1", 0), ("g0", 1)], 16) for i in range(GH)]
        stored = [Signal(sem(f"stored{i}"), [("out", -2)], 16) for i in range(2)]
        const_loaded = sem("const_loaded")
        ident_made = sem("ident_made")
        setup_pe, setup_act, setup_dve = sem("setup_pe"), sem("setup_act"), sem("setup_dve")

        def f(ap):
            return ap.bitcast(F32)

        def rows(dram, b, c0=0, c1=NT):
            return dram[bass.ds(b, 1), c0 * P:c1 * P, :].rearrange("a (c p) d -> p (a c) d", p=P)

        block = ctx.enter_context(nc.Block())

        def program(engine, iteration):
            for t in range(FIRST, LOOP_FROM):
                iteration(t, t % 2)
            with engine.Fori(LOOP_FROM // 2, LOOP_TO // 2) as pair:
                iteration(2 * pair, 0)
                iteration(2 * pair + 1, 1)
            for t in range(LOOP_TO, LAST + 1):
                iteration(t, t % 2)

        @block.sync
        def _(sp):
            n = 0
            for k, w in enumerate((wq, wk, wv, wo)):
                sp.dma_start(z[:, k, :].rearrange("p (o i) -> p o i", o=DT),
                             w.rearrange("(o p) i -> p o i", p=P)).then_inc(const_loaded, 16)
            sp.dma_start(h[0][:, 0:DT, :], fc_w.rearrange("(o p) i -> p o i", p=P)).then_inc(const_loaded, 16)
            for k, b in enumerate((bq, bk, bv)):
                sp.dma_start(bias_col[:, k, :], b.rearrange("(g p) -> p g", p=P),
                             allow_slow_non_contiguous=True).then_inc(const_loaded, 16)
            sp.dma_start(kw_col[:, :], k_w.rearrange("a (g p) -> p (a g)", p=P),
                         allow_slow_non_contiguous=True).then_inc(const_loaded, 16)
            for row, b in ((gamma_row, gamma), (beta_row, beta), (bo_row, bo), (fcb_row, fc_b)):
                sp.dma_start(row[:, :], b.partition_broadcast(P)).then_inc(const_loaded, 16)
            for row, b in ((qw_row[:, :], q_w), (zt[:, 2, 0:D], k_w)):
                sp.dma_start(row, b.rearrange("a d -> (a d)").partition_broadcast(P)).then_inc(const_loaded, 16)
            for k, b in enumerate((q_b, k_b)):
                sp.dma_start(qkb[:, k:k + 1], b.partition_broadcast(P)).then_inc(const_loaded, 16)
            sp.dma_start(x_in[:, :, :], rows(x, 0)).then_inc(x_loaded.sem, 16)

            def stack(g, t):
                sp.wait_ge(dve_done.sem, dve_done.after(f"k_lo{g}", t if g == 0 else t - 1))
                sp.nop(nofuse=True)
                for i in range(GH):
                    r = slice(DH * i, DH * (i + 1))
                    for part, (q_part, k_part) in enumerate(((qt_hi, kt_hi), (qt_lo, kt_hi), (qt_hi, kt_lo))):
                        to = slice(DH * part, DH * (part + 1))
                        sp.dma_start(f(q_stack[g][to, i, :]), f(q_part[g][r, :])).then_inc(stacked[g].sem, 16)
                        sp.dma_start(f(k_stack[g][to, i, :]), f(k_part[g][r, :])).then_inc(stacked[g].sem, 16)

            def place_max(j, t):
                g, i = j // GH, j % GH
                sp.wait_ge(dve_done.sem, dve_done.after(f"m{j}", t))
                sp.nop(nofuse=True)
                sp.dma_start(f(q_stack[g][STACK:STACK + 1, i, :]), f(neg_max[:, j % 2, :])).then_inc(max_placed[i].sem, 16)

            def iteration(t, par):
                if on(t, 1):
                    sp.wait_ge(dve_done.sem, dve_done.after("l_max3", t - 1))
                    sp.nop(nofuse=True)
                    sp.dma_start(adj_in[:, :, :], rows(adj, t + 1)).then_inc(adj_loaded.sem, 16)
                if on(t, 0):
                    sp.wait_ge(st_done.sem, st_done.after(POS - 1, t - 1))
                    sp.nop(nofuse=True)
                    stack(1, t)
                    place_max(4, t)
                    place_max(5, t)
                if on(t, -1):
                    sp.wait_ge(pool_done.sem, pool_done.after("diag", t))
                    sp.nop(nofuse=True)
                    sp.wait_ge(dve_done.sem, dve_done.after("l_max3", t - 1))
                    sp.nop(nofuse=True)
                    sp.dma_start(adj_in[:, :, :], rows(adj, t - 1)).then_inc(adj_loaded.sem, 16)
                if on(t, 0):
                    place_max(6, t)
                for half in range(2):
                    if on(t, -2):
                        sp.wait_ge(dve_done.sem, dve_done.after(f"fin{half}", t))
                        sp.nop(nofuse=True)
                        c = 2 * half
                        sp.dma_start(rows(out, t - 2, c, c + 2), h[par][:, c:c + 2, :]).then_inc(stored[half].sem, 16)
                if on(t, 0):
                    place_max(7, t)
                if on(t, 1):
                    sp.wait_ge(st_done.sem, st_done.after(POS // 2 - 1, t))
                    sp.nop(nofuse=True)
                    stack(0, t)
                    place_max(0, t)
                if on(t, 0):
                    for half in range(2):
                        sp.wait_ge(stored[half].sem, stored[half].after("out", t))
                        sp.nop(nofuse=True)
                    sp.dma_start(h[par][:, :, :], rows(x, t)).then_inc(h_loaded.sem, 16)
                if on(t, 1):
                    place_max(1, t)
                    place_max(2, t)
                if on(t, 2):
                    sp.wait_ge(pe_done.sem, pe_done.after("xt1", t))
                    sp.nop(nofuse=True)
                    sp.wait_ge(dve_done.sem, dve_done.after("o_lo0", t))
                    sp.nop(nofuse=True)
                    sp.dma_start(x_in[:, :, :], rows(x, t + 2)).then_inc(x_loaded.sem, 16)
                if on(t, 1):
                    place_max(3, t)

            sp.wait_ge(setup_pe, 6)
            program(sp, iteration)
            for half in range(2):
                sp.wait_ge(stored[half].sem, stored[half].after("out", LAST))
                sp.nop(nofuse=True)

        @block.tensor
        def _(pe):
            N_CONST = 17
            pe.wait_ge(ident_made, 9)
            pe.wait_ge(const_loaded, 16 * N_CONST)
            setup_banks = [*shared, *sm_bank, o_bank]
            for k in range(5):
                for i in range(DT):
                    for o in range(DT):
                        src = z[:, k, o * D + i * P:o * D + (i + 1) * P] if k < 4 else h[0][:, o, i * P:(i + 1) * P]
                        last = nc.tensor.transpose(setup_banks[k][:, (i * DT + o) * P:(i * DT + o + 1) * P],
                                                   src, ident[:, :])
                last.then_inc(setup_pe, 1)
            pe.wait_ge(setup_dve, 1)
            for i in range(DT):
                for o in range(DT):
                    last = nc.tensor.matmul(setup_banks[5][:, i * P:(i + 1) * P], h[0][:, o, i * P:(i + 1) * P],
                                            zt[:, 0, o * P:(o + 1) * P], start=(o == 0), stop=(o == DT - 1))
            last.then_inc(setup_pe, 1)
            pe.wait_ge(setup_dve, 8)

            def bank_read(name, t):
                other, tb = name, t
                while True:
                    other, earlier = before[other]
                    tb = tb - 1 if earlier else tb
                    if on(tb, OFF[other]) or tb < FIRST:
                        break
                who, reader = READ_BY[other]
                return made[who].sem, made[who].after(reader, tb)

            def three_terms(bank, terms, kts=DT):
                for kt in range(kts):
                    (ah, al), (bh, bl) = terms(kt)
                    for n, (a, b) in enumerate(((ah, bh), (ah, bl), (al, bh))):
                        last = nc.tensor.matmul(bank, a, b, start=(kt == 0 and n == 0), stop=(kt == kts - 1 and n == 2))
                return last

            def iteration(t, par):
                nxt = 1 - par

                def turn_x(kt):
                    if kt == 0:
                        pe.wait_ge(x_loaded.sem, x_loaded.after("x", t - 1))
                    pe.wait_ge(*bank_read(f"xt{kt}", t))
                    bank = bank_of[f"xt{kt}"]
                    for c in range(NT):
                        last = nc.tensor.transpose(bank[:, c * P:(c + 1) * P], x_in[:, c, kt * P:(kt + 1) * P], ident[:, :])
                    last.then_inc(pe_done.sem, 1)

                def project_qk(name, w, g):
                    pe.wait_ge(dve_done.sem, dve_done.after("x_lo1", t))
                    pe.wait_ge(*bank_read(f"{name}{g}", t))
                    bank = bank_of[f"{name}{g}"]
                    o = slice(g * P, (g + 1) * P)
                    three_terms(bank[:, :], lambda kt: ((weight_hi[:, w, kt, o], weight_lo[:, w, kt, o]),
                                                        (xt_hi[:, kt, :], xt_lo[:, kt, :]))).then_inc(pe_done.sem, 1)

                def rows_times(name, half, hi, lo, w):
                    pe.wait_ge(*bank_read(f"{name}{half}", t))
                    bank = bank_of[f"{name}{half}"]
                    for k in range(2):
                        n = slice((2 * half + k) * P, (2 * half + k + 1) * P)
                        last = three_terms(bank[:, k * D:(k + 1) * D],
                                           lambda kt: ((hi[:, kt, n], lo[:, kt, n]),
                                                       (weight_hi[:, w, kt, :], weight_lo[:, w, kt, :])))
                    last.then_inc(pe_done.sem, 1)

                def out_project(half):
                    if half == 0:
                        pe.wait_ge(dve_done.sem, dve_done.after("o_lo1", t))
                    rows_times("op", half, o_hi, o_lo, WO)

                def fc_project(half):
                    if half == 0:
                        pe.wait_ge(dve_done.sem, dve_done.after("h_lo1", t))
                    rows_times("fc", half, ht_hi, ht_lo, FC)

                def turn_mask(half):
                    if half == 0:
                        pe.wait_ge(pool_done.sem, pool_done.after("diag", t))
                    pe.wait_ge(*bank_read(f"mt{half}", t))
                    bank = bank_of[f"mt{half}"][:, :].bitcast(BF16)
                    for k in range(2):
                        for c in range(NT):
                            key = (2 * half + k) * P
                            last = nc.tensor.transpose(bank[:, k * N + c * P:k * N + (c + 1) * P],
                                                       mask[nxt][:, c * N + key:c * N + key + P], ident_b[:, :])
                    last.then_inc(pe_done.sem, 1)

                def turn_max(j):
                    pe.wait_ge(max_done.sem, max_done.after((4 * j + 15) % POS, t if j < 4 else t - (1 if 4 * j + 15 < POS else 0)))
                    pe.wait_ge(*bank_read(f"m{j}", t))
                    bank = bank_of[f"m{j}"]
                    nc.tensor.transpose(bank[0:NT, 0:P], row_max[:, j, :], ident[:, :]).then_inc(pe_done.sem, 1)

                def times_v(k):
                    kt = (k - 1) % NT
                    g, vv = (1, v[nxt]) if k == 0 else ((k - 1) // NT, v[par])
                    pe.wait_ge(exp_done.sem, exp_done.after((4 * k - 1) % POS, t if k else t - 1))
                    if k == 1:
                        pe.wait_ge(act_done.sem, act_done.after("v1", t - 1))
                    if kt == 0:
                        pe.wait_ge(act_done.sem, act_done.after(f"o_raw{1 - g}", t))
                    for i in range(GH):
                        o = g * P + i * DH
                        last = nc.tensor.matmul(o_bank[i * DH:(i + 1) * DH, :], vv[:, kt, o:o + DH], e[:, kt, i, :],
                                                start=(kt == 0), stop=(kt == NT - 1))
                    last.then_inc(pe_done.sem, 1)

                def total(g):
                    pe.wait_ge(pool_done.sem, pool_done.after(f"sum{g}_3", t))
                    pe.wait_ge(*bank_read(f"sum{g}", t))
                    bank = bank_of[f"sum{g}"]
                    for i in range(GH):
                        last = nc.tensor.matmul(bank[i * DH:(i + 1) * DH, :], ones[:, :], e_sum[:, i, :], start=True, stop=True)
                    last.then_inc(pe_done.sem, 1)

                def turn_h(kt):
                    if kt == 0:
                        pe.wait_ge(dve_done.sem, dve_done.after("h_b", t))
                    pe.wait_ge(*bank_read(f"ht{kt}", t))
                    bank = bank_of[f"ht{kt}"]
                    for c in range(NT):
                        last = nc.tensor.transpose(bank[:, c * P:(c + 1) * P], h[nxt][:, c, kt * P:(kt + 1) * P], ident[:, :])
                    last.then_inc(pe_done.sem, 1)

                def key_logits():
                    pe.wait_ge(*bank_read("kb", t))
                    bank = bank_of["kb"]
                    three_terms(bank[:, :], lambda kt: ((uk_hi[:, kt, :], uk_lo[:, kt, :]),
                                                        (ht_hi[:, kt, :], ht_lo[:, kt, :]))).then_inc(pe_done.sem, 1)

                def turn_z(c):
                    pe.wait_ge(act_done.sem, act_done.after(f"lexp{c}", t))
                    pe.wait_ge(*bank_read(f"et{c}", t))
                    bank = bank_of[f"et{c}"]
                    for k in range(NT):
                        last = nc.tensor.transpose(bank[:, k * P:(k + 1) * P], z[:, c, k * P:(k + 1) * P], ident[:, :])
                    last.then_inc(pe_done.sem, 1)

                def attend(c):
                    half, k = c // 2, c % 2
                    if c == 0:
                        pe.wait_ge(act_done.sem, act_done.after("et3", t))
                    if k == 0:
                        pe.wait_ge(*bank_read(f"at{half}", t))
                    bank = bank_of[f"at{half}"]
                    for kt in range(NT):
                        last = nc.tensor.matmul(bank[:, k * D:(k + 1) * D], zt[:, kt, c * P:(c + 1) * P], feat[:, kt, :],
                                                start=(kt == 0), stop=(kt == NT - 1))
                    if k == 1:
                        last.then_inc(pe_done.sem, 1)

                for s in range(POS):
                    g, kt, i = s // (POS // 2), s // GH % NT, s % GH
                    if on(t, 0):
                        if kt == 0 and i == 0:
                            pe.wait_ge(stacked[g].sem, stacked[g].after(f"g{g}", t if g else t - 1))
                            if g == 0:
                                pe.wait_ge(act_done.sem, act_done.after("mt1", t - 1))
                        if kt == 0:
                            pe.wait_ge(max_placed[i].sem, max_placed[i].after(f"g{g}", t if g else t - 1))
                        pe.wait_ge(exp_done.sem, exp_done.after((s - 2) % POS, t if s >= 2 else t - 1))
                        bank = st_bank[s % 2]
                        nc.tensor.matmul(bank[:, :], k_stack[g][:, i, kt * P:(kt + 1) * P], q_stack[g][:, i, :],
                                         start=True, stop=False)
                        nc.tensor.matmul(bank[:, :], ident_b[:, :], mask_t[par][:, kt, :],
                                         start=False, stop=True).then_inc(st_done.sem, 1)
                    off, j, qt = maxima_tile(s)
                    if on(t, off):
                        if j % GH == 0 and qt == 0:
                            pe.wait_ge(act_done.sem, act_done.after(f"k_hi{j // GH}", t))
                        pe.wait_ge(max_done.sem, max_done.after((s - 2) % POS, t if s >= 2 else t - 1))
                        r = slice(DH * (j % GH), DH * (j % GH + 1))
                        nc.tensor.matmul(sm_bank[s % 2][:, :], qt_hi[j // GH][r, qt * P:(qt + 1) * P],
                                         kt_hi[j // GH][r, :], start=True, stop=True).then_inc(sm_done.sem, 1)
                    if s == 1:
                        if on(t, 1):
                            turn_x(0)
                    if s == 2:
                        if on(t, 1):
                            turn_x(1)
                        if on(t, 0):
                            turn_max(4)
                        if on(t, -1):
                            times_v(0)
                    if s == 3:
                        if on(t, -2):
                            turn_z(0)
                    if s == 4:
                        if on(t, -2):
                            turn_z(1)
                        if on(t, 1):
                            project_qk("q", WQ, 0)
                    if s == 5:
                        if on(t, 1):
                            project_qk("k", WK, 0)
                    if s == 6:
                        if on(t, -2):
                            turn_z(2)
                        if on(t, 0):
                            turn_max(5)
                            times_v(1)
                    if s == 7:
                        if on(t, -2):
                            turn_z(3)
                    if s == 8:
                        if on(t, -1):
                            total(1)
                    if s == 9:
                        if on(t, -2):
                            attend(0)
                    if s == 10:
                        if on(t, 0):
                            turn_max(6)
                            times_v(2)
                        if on(t, -2):
                            attend(1)
                    if s == 11:
                        if on(t, -2):
                            attend(2)
                    if s == 12:
                        if on(t, -2):
                            attend(3)
                    if s == 13:
                        if on(t, -1):
                            out_project(0)
                    if s == 14:
                        if on(t, 0):
                            turn_max(7)
                            times_v(3)
                    if s == 15:
                        if on(t, -1):
                            out_project(1)
                    if s == 16:
                        if on(t, 1):
                            turn_mask(0)
                    if s == 17:
                        if on(t, 1):
                            turn_mask(1)
                    if s == 18:
                        if on(t, 1):
                            turn_max(0)
                        if on(t, 0):
                            times_v(4)
                    if s == 19:
                        if on(t, 1):
                            project_qk("q", WQ, 1)
                    if s == 21:
                        if on(t, 1):
                            project_qk("k", WK, 1)
                    if s == 22:
                        if on(t, 1):
                            turn_max(1)
                        if on(t, 0):
                            times_v(5)
                        if on(t, -1):
                            turn_h(0)
                    if s == 23:
                        if on(t, -1):
                            turn_h(1)
                    if s == 24:
                        if on(t, 0):
                            total(0)
                    if s == 25:
                        if on(t, -1):
                            fc_project(0)
                    if s == 26:
                        if on(t, 1):
                            turn_max(2)
                        if on(t, 0):
                            times_v(6)
                    if s == 27:
                        if on(t, -1):
                            fc_project(1)
                    if s == 28:
                        if on(t, -1):
                            key_logits()
                    if s == 29:
                        if on(t, 1):
                            rows_times("v", 0, xt_hi, xt_lo, WV)
                    if s == 30:
                        if on(t, 1):
                            turn_max(3)
                        if on(t, 0):
                            times_v(7)
                    if s == 31:
                        if on(t, 1):
                            rows_times("v", 1, xt_hi, xt_lo, WV)

            program(pe, iteration)

        @block.scalar
        def _(act):
            for k in range(5):
                act.wait_ge(setup_pe, k + 1)
                bank = [*shared, *sm_bank][k]
                nc.scalar.copy(weight_hi[:, k, :, :], bank[:, :].rearrange("p (i o) -> p i o", i=DT)).then_inc(setup_act, 1)
            act.wait_ge(setup_pe, 6)
            nc.scalar.copy(uk_hi[:, :, :], o_bank[:, 0:DT * P].rearrange("p (i o) -> p i o", i=DT)).then_inc(setup_act, 1)
            act.wait_ge(const_loaded, 16 * 17)

            def iteration(t, par):
                nxt = 1 - par

                def logits(c):
                    act.wait_ge(dve_done.sem, dve_done.after("l_max1" if c < 2 else "l_max3", t))
                    nc.scalar.activation(z[:, c, :], z[:, c, :], ACT.Identity, bias=q_bias[:, c:c + 1])\
                        .then_inc(act_done.sem, 1)

                def exponentials(c):
                    act.wait_ge(dve_done.sem, dve_done.after(f"leaky{c}", t - 1 if c == 0 else t))
                    nc.scalar.activation(z[:, c, :], z[:, c, :], ACT.Exp, bias=l_negmax[:, c:c + 1],
                                         accum_out=l_sum[:, c:c + 1]).then_inc(act_done.sem, 1)

                def copy(dst, name, bank_ap):
                    act.wait_ge(pe_done.sem, pe_done.after(name, t))
                    nc.scalar.copy(dst, bank_ap).then_inc(act_done.sem, 1)

                def turned_z(c):
                    copy(zt[:, :, c * P:(c + 1) * P], f"et{c}",
                         bank_of[f"et{c}"][:, :].rearrange("p (k n) -> p k n", k=NT))

                def values(half):
                    copy(v[nxt][:, 2 * half:2 * half + 2, :], f"v{half}",
                         bank_of[f"v{half}"][:, :].rearrange("p (k n) -> p k n", k=2))

                def turned_mask(half):
                    copy(mask_t[nxt][:, 2 * half:2 * half + 2, :], f"mt{half}",
                         bank_of[f"mt{half}"][:, :].bitcast(BF16).rearrange("p (k n) -> p k n", k=2))

                def qk_high(name, dst, k, g):
                    act.wait_ge(pe_done.sem, pe_done.after(f"{name}{g}", t))
                    act.wait_ge(stacked[g].sem, stacked[g].after(f"g{g}", t - 1 if g == 0 else t))
                    nc.scalar.activation(dst[g][:, :], bank_of[f"{name}{g}"][:, :], ACT.Identity,
                                         bias=bias_col[:, k, g:g + 1]).then_inc(act_done.sem, 1)

                def o_high(g):
                    act.wait_ge(dve_done.sem, dve_done.after(f"o_norm{g}", t))
                    nc.scalar.activation(o_hi[:, g, :], o_raw, ACT.Identity,
                                         bias=bias_col[:, 2, g:g + 1]).then_inc(act_done.sem, 1)

                for s in range(POS):
                    g, kt, i = s // (POS // 2), s // GH % NT, s % GH
                    if on(t, 0):
                        act.wait_ge(st_done.sem, st_done.after(s, t))
                        if i == 0:
                            n = max(kt, 1)
                            if g == 1:
                                act.wait_ge(pe_done.sem, pe_done.after(f"pv{kt + 1}", t))
                                act.wait_ge(pool_done.sem, pool_done.after(f"sum0_{n}", t))
                            elif kt < NT - 1:
                                act.wait_ge(pe_done.sem, pe_done.after(f"pv{kt + 5}", t - 1))
                                act.wait_ge(pool_done.sem, pool_done.after(f"sum1_{n}", t - 1))
                            else:
                                act.wait_ge(pe_done.sem, pe_done.after("pv0", t))
                                act.wait_ge(pool_done.sem, pool_done.after("sum1_3", t))
                        nc.scalar.activation(e[:, kt, i, :], st_bank[s % 2][:, :], ACT.Exp, scale=SCALE)\
                            .then_inc(exp_done.sem, 1)
                    if s in (0, 1) and on(t, -2):
                        exponentials(s)
                    if s in (2, 3) and on(t, 1):
                        copy(xt_hi[:, s - 2, :], f"xt{s - 2}", bank_of[f"xt{s - 2}"][:, :])
                    if s == 3 and on(t, -1):
                        copy(o_raw, "pv0", o_bank[:, :])
                    if s in (2, 3) and on(t, -2):
                        exponentials(s)
                    if s == 4 and on(t, -2):
                        turned_z(0)
                    if s == 5 and on(t, 1):
                        qk_high("q", qt_hi, 0, 0)
                    if s == 5 and on(t, -2):
                        turned_z(1)
                    if s == 6 and on(t, 1):
                        qk_high("k", kt_hi, 1, 0)
                    if s in (7, 8) and on(t, -2):
                        turned_z(s - 5)
                    if s == 8 and on(t, -1):
                        copy(recip, "sum1", bank_of["sum1"][:, :])
                    if s == 11 and on(t, -1):
                        o_high(1)
                    if s in (17, 18) and on(t, 1):
                        turned_mask(s - 17)
                    if s == 19 and on(t, 0):
                        copy(o_raw, "pv4", o_bank[:, :])
                    if s == 20 and on(t, 1):
                        qk_high("q", qt_hi, 0, 1)
                    if s == 22 and on(t, 1):
                        qk_high("k", kt_hi, 1, 1)
                    if s in (23, 24) and on(t, -1):
                        copy(ht_hi[:, s - 23, :], f"ht{s - 23}", bank_of[f"ht{s - 23}"][:, :])
                    if s == 25 and on(t, 0):
                        copy(recip, "sum0", bank_of["sum0"][:, :])
                    if s in (26, 28) and on(t, -1):
                        half = (s - 26) // 2
                        copy(feat[:, 2 * half:2 * half + 2, :], f"fc{half}",
                             bank_of[f"fc{half}"][:, :].rearrange("p (k n) -> p k n", k=2))
                    if s == 27 and on(t, 0):
                        o_high(0)
                    if s == 30 and on(t, 1):
                        values(0)
                    if s in (30, 31) and on(t, -1):
                        logits(2 * (s - 30))
                        logits(2 * (s - 30) + 1)
                    if s == 31 and on(t, 1):
                        values(1)

            program(act, iteration)

        @block.vector
        def _(dve):
            dve.wait_ge(const_loaded, 16 * 17)
            dve.wait_ge(ident_made, 9)
            for o in range(DT):
                last = nc.vector.tensor_scalar(zt[:, 0, o * P:(o + 1) * P], zt[:, 1, 0:P], kw_col[:, o:o + 1], None, ALU.add)
            last.then_inc(setup_dve, 1)
            for k, row in enumerate((qw_row[:, :], zt[:, 2, 0:D])):
                last = nc.vector.tensor_tensor_reduce(zt[:, 3, k * D:(k + 1) * D], fcb_row[:, :], row, 1.0, 0.0, ALU.mult, ALU.add,
                                                      logit_bias[:, k:k + 1])
            for k in range(6):
                dve.wait_ge(setup_act, k + 1)
                hi, lo = (weight_hi[:, k, :, :], weight_lo[:, k, :, :]) if k < 5 else (uk_hi[:, :, :], uk_lo[:, :, :])
                bank = [*shared, *sm_bank, o_bank][k][:, 0:512 if k < 5 else DT * P]
                nc.vector.tensor_tensor(lo, bank.rearrange("p (i o) -> p i o", i=DT), f(hi), ALU.subtract).then_inc(setup_dve, 1)
            dve.wait_ge(setup_dve, 7)
            nc.vector.tensor_tensor(logit_bias[:, 0:2], logit_bias[:, 0:2], qkb[:, :], ALU.add).then_inc(setup_dve, 1)
            dve.wait_ge(setup_dve, 8)
            nc.vector.tensor_tensor(logit_bias[:, 3:4], logit_bias[:, 0:1], logit_bias[:, 1:2], ALU.add).then_inc(setup_dve, 1)
            dve.wait_ge(setup_dve, 9)

            def iteration(t, par):
                nxt = 1 - par
                done = dve_done.sem

                def lo_part(dst, name, hi_ready, hi):
                    dve.wait_ge(act_done.sem, act_done.after(hi_ready, t))
                    nc.vector.tensor_tensor(dst, bank_of[name][:, :], f(hi), ALU.subtract).then_inc(done, 1)

                def qk_lo(name, g, k, dst, hi):
                    dve.wait_ge(act_done.sem, act_done.after(f"{name}_hi{g}", t))
                    nc.vector.scalar_tensor_tensor(dst[g][:, :], bank_of[f"{name}{g}"][:, :], bias_col[:, k, g:g + 1],
                                                   f(hi[g][:, :]), ALU.add, ALU.subtract).then_inc(done, 1)

                def negate_max(j):
                    dve.wait_ge(pe_done.sem, pe_done.after(f"m{j}", t))
                    i2, g2 = (j - 2) % GH, (j - 2) % NH // GH
                    tb = t - 1 if j in (4, 5) else t
                    dve.wait_ge(max_placed[i2].sem, max_placed[i2].after(f"g{g2}", tb))
                    nc.vector.tensor_scalar(neg_max[:, j % 2, :], bank_of[f"m{j}"][0:NT, 0:P], -1.0, None, ALU.mult)\
                        .then_inc(done, 1)

                def reciprocals(g, quarters):
                    if quarters[0] == 0:
                        dve.wait_ge(act_done.sem, act_done.after(f"sum{g}", t))
                    for k in quarters:
                        last = nc.vector.reciprocal(recip[:, k * P:(k + 1) * P], recip[:, k * P:(k + 1) * P])
                    if quarters[-1] == NT - 1:
                        last.then_inc(done, 1)

                def normalise(g):
                    dve.wait_ge(act_done.sem, act_done.after(f"o_raw{g}", t))
                    dve.wait_ge(dve_done.sem, dve_done.after(f"recip{g}", t))
                    nc.vector.tensor_tensor(o_raw, o_raw, recip, ALU.mult).then_inc(done, 1)

                def o_low(g):
                    dve.wait_ge(act_done.sem, act_done.after(f"o_hi{g}", t))
                    nc.vector.scalar_tensor_tensor(o_lo[:, g, :], o_raw, bias_col[:, 2, g:g + 1], f(o_hi[:, g, :]),
                                                   ALU.add, ALU.subtract).then_inc(done, 1)

                def finish(half):
                    dve.wait_ge(pe_done.sem, pe_done.after(f"at{half}", t))
                    if half == 0:
                        dve.wait_ge(dve_done.sem, dve_done.after("l_recip", t))
                    for k in range(2):
                        c = 2 * half + k
                        last = nc.vector.scalar_tensor_tensor(h[par][:, c, :], bank_of[f"at{half}"][:, k * D:(k + 1) * D],
                                                              l_recip[:, c:c + 1], h[par][:, c, :], ALU.mult, ALU.add)
                    last.then_inc(done, 1)

                def add_residual(half):
                    dve.wait_ge(pe_done.sem, pe_done.after(f"op{half}", t))
                    if half == 0:
                        dve.wait_ge(pool_done.sem, pool_done.after("x_bo", t))
                    hc = h[nxt][:, 2 * half:2 * half + 2, :]
                    nc.vector.tensor_tensor(hc, bank_of[f"op{half}"][:, :].rearrange("p (k n) -> p k n", k=2), hc, ALU.add)\
                        .then_inc(done, 1)

                def query_logits(half):
                    dve.wait_ge(act_done.sem, act_done.after(f"feat{half}", t))
                    if half == 0:
                        dve.wait_ge(pe_done.sem, pe_done.after("et3", t))
                    for k in range(2):
                        c = 2 * half + k
                        last = nc.vector.tensor_tensor_reduce(z[:, c, 0:D], feat[:, c, :], qw_row[:, :], 1.0, 0.0,
                                                              ALU.mult, ALU.add, q_dot[:, c:c + 1])
                    last.then_inc(done, 1)

                def leaky(c):
                    dve.wait_ge(act_done.sem, act_done.after(f"logit{c}", t if c == 0 else t - 1))
                    nc.vector.scalar_tensor_tensor(z[:, c, :], z[:, c, :], SLOPE, z[:, c, :], ALU.mult, ALU.max)\
                        .then_inc(done, 1)

                def layer1_maxima(half):
                    if half == 0:
                        dve.wait_ge(pe_done.sem, pe_done.after("kb", t))
                        dve.wait_ge(pool_done.sem, pool_done.after("l_mask", t))
                        dve.nop(nofuse=True)
                    for k in range(2):
                        c = 2 * half + k
                        last = nc.vector.tensor_tensor_reduce(z[:, c, :], bank_of["kb"][:, :], adj_in[:, c, :], 1.0, LOWEST,
                                                              ALU.add, ALU.max, l_max[:, c:c + 1])
                    last.then_inc(done, 1)

                for s in range(POS):
                    off, j, qt = maxima_tile(s)
                    if on(t, off):
                        if off == 1 and j == 0 and qt == 0:
                            dve.wait_ge(pool_done.sem, pool_done.after("diag", t))
                        dve.wait_ge(sm_done.sem, sm_done.after(s, t))
                        dve.nop(nofuse=True)
                        nc.vector.tensor_tensor_reduce(sm_bank[s % 2][:, :], sm_bank[s % 2][:, :],
                                                       mask[nxt if off else par][:, qt * N:(qt + 1) * N], 1.0, LOWEST,
                                                       ALU.add, ALU.max, row_max[:, j, qt:qt + 1]).then_inc(max_done.sem, 1)
                    if s in (0, 1) and on(t, -2):
                        leaky(s + 1)
                    if s in (2, 3) and on(t, 1):
                        lo_part(xt_lo[:, s - 2, :], f"xt{s - 2}", f"x_hi{s - 2}", xt_hi[:, s - 2, :])
                    if s == 2 and on(t, -2):
                        leaky(3)
                    if s == 3 and on(t, 0):
                        negate_max(4)
                    if s == 5 and on(t, 1):
                        qk_lo("q", 0, 0, qt_lo, qt_hi)
                    if s == 6 and on(t, 1):
                        qk_lo("k", 0, 1, kt_lo, kt_hi)
                    if s == 7 and on(t, 0):
                        negate_max(5)
                    if s == 7 and on(t, 1):
                        dve.wait_ge(adj_loaded.sem, adj_loaded.after("adj", t))
                        nc.vector.tensor_scalar(mask[nxt], adj_in[:, :, :].rearrange("p c n -> p (c n)"),
                                                0.0, -BIG, ALU.is_le, ALU.mult).then_inc(done, 1)
                    if s in (9, 10) and on(t, -1):
                        reciprocals(1, (0, 1) if s == 9 else (2, 3))
                    if s == 11 and on(t, 0):
                        negate_max(6)
                    if s == 11 and on(t, -1):
                        normalise(1)
                    if s == 11 and on(t, -2):
                        dve.wait_ge(act_done.sem, act_done.after("lexp3", t))
                        nc.vector.reciprocal(l_recip[:, :], l_sum[:, :]).then_inc(done, 1)
                        dve.wait_ge(pool_done.sem, pool_done.after("h_fcb", t - 1))
                        finish(0)
                    if s == 12 and on(t, -1):
                        o_low(1)
                    if s == 13 and on(t, -2):
                        finish(1)
                    if s == 14 and on(t, -1):
                        add_residual(0)
                    if s == 15 and on(t, 0):
                        negate_max(7)
                    if s == 16 and on(t, -1):
                        add_residual(1)
                        dve.wait_ge(dve_done.sem, dve_done.after("h_add1", t))
                        for c in range(NT):
                            last = nc.vector.bn_stats(stats[:, c, :], h[nxt][:, c, :])
                        last.then_inc(done, 1)
                    if s == 17 and on(t, -1):
                        dve.wait_ge(dve_done.sem, dve_done.after("stats", t))
                        dve.nop(nofuse=True)
                        for c in range(NT):
                            last = nc.vector.bn_aggr(moments[:, c, :], stats[:, c, :])
                        last.then_inc(done, 1)
                        dve.wait_ge(dve_done.sem, dve_done.after("moments", t))
                        nc.vector.tensor_scalar(var_eps[:, :], moments[:, :, 1], EPS, None, ALU.add).then_inc(done, 1)
                        for c in range(NT):
                            last = nc.vector.scalar_tensor_tensor(h[nxt][:, c, :], h[nxt][:, c, :], moments[:, c, 0:1],
                                                                  gamma_row[:, :], ALU.subtract, ALU.mult)
                        last.then_inc(done, 1)
                    if s == 19 and on(t, 1):
                        negate_max(0)
                    if s == 20 and on(t, 1):
                        qk_lo("q", 1, 0, qt_lo, qt_hi)
                    if s in (20, 21) and on(t, -1):
                        if s == 20:
                            dve.wait_ge(pool_done.sem, pool_done.after("rstd", t))
                            dve.wait_ge(dve_done.sem, dve_done.after("centre", t))
                        for c in range(2 * (s - 20), 2 * (s - 20) + 2):
                            last = nc.vector.scalar_tensor_tensor(h[nxt][:, c, :], h[nxt][:, c, :], rstd[:, c:c + 1],
                                                                  beta_row[:, :], ALU.mult, ALU.add)
                        last.then_inc(done, 1)
                    if s == 22 and on(t, 1):
                        qk_lo("k", 1, 1, kt_lo, kt_hi)
                    if s == 23 and on(t, 1):
                        negate_max(1)
                    if s in (23, 24) and on(t, -1):
                        lo_part(ht_lo[:, s - 23, :], f"ht{s - 23}", f"h_hi{s - 23}", ht_hi[:, s - 23, :])
                    if s in (25, 26) and on(t, 0):
                        reciprocals(0, (0, 1) if s == 25 else (2, 3))
                    if s == 27 and on(t, 1):
                        negate_max(2)
                    if s == 27 and on(t, 0):
                        normalise(0)
                    if s == 27 and on(t, -1):
                        query_logits(0)
                    if s == 28 and on(t, -1):
                        query_logits(1)
                        dve.wait_ge(dve_done.sem, dve_done.after("q_dot1", t))
                        nc.vector.tensor_scalar(q_bias[:, :], q_dot[:, :], logit_bias[:, 3:4], None, ALU.add).then_inc(done, 1)
                    if s == 28 and on(t, 0):
                        o_low(0)
                    if s == 29 and on(t, -1):
                        layer1_maxima(0)
                    if s == 30 and on(t, -1):
                        layer1_maxima(1)
                    if s == 31 and on(t, 1):
                        negate_max(3)
                    if s == 31 and on(t, -1):
                        dve.wait_ge(dve_done.sem, dve_done.after("l_max3", t))
                        nc.vector.tensor_tensor(l_z[:, :], l_max[:, :], q_bias[:, :], ALU.add).then_inc(done, 1)
                        dve.wait_ge(dve_done.sem, dve_done.after("l_z", t))
                        nc.vector.tensor_scalar(l_nz[:, :], l_z[:, :], -1.0, None, ALU.mult).then_inc(done, 1)
                        dve.wait_ge(dve_done.sem, dve_done.after("l_nz", t))
                        nc.vector.scalar_tensor_tensor(l_negmax[:, :], l_nz[:, :], SLOPE, l_nz[:, :], ALU.mult, ALU.min)\
                            .then_inc(done, 1)
                        leaky(0)

            program(dve, iteration)

        @block.gpsimd
        def _(pool):
            for ap in (ident, ident_b):
                nc.gpsimd.memset(ap[:, :], 0.0).then_inc(ident_made, 1)
            pool.wait_ge(ident_made, 2)
            for ap in (ident, ident_b):
                nc.gpsimd.affine_select(out=ap[:, :], in_=ap[:, :], compare_op=ALU.not_equal, fill=1.0, base=0,
                                        pattern=[[-1, P]], channel_multiplier=1).then_inc(ident_made, 1)
            for n, (ap, value) in enumerate((*((f(k_stack[g][STACK:STACK + 1, :, :]), 1.0) for g in range(NG)),
                                             (minus_half[:, :], -0.5), (zt[:, 1, 0:P], 0.0), (ones[:, :], 1.0))):
                pool.wait_ge(ident_made, 4 + n)
                nc.gpsimd.memset(ap, value).then_inc(ident_made, 1)
            pool.wait_ge(const_loaded, 16 * 17)

            def iteration(t, par):
                nxt = 1 - par

                def add_e(g, n):
                    slot = (g * NT + n) * GH + GH - 1
                    tb = t if (g, n) != (1, 3) else t - 1
                    pool.wait_ge(exp_done.sem, exp_done.after(slot, tb))
                    if n == 1:
                        pool.wait_ge(pe_done.sem, pe_done.after(f"sum{1 - g}", t))
                        a, b = e[:, 0, :, :], e[:, 1, :, :]
                    else:
                        pool.wait_ge(pool_done.sem, pool_done.after(f"sum{g}_{n - 1}", tb))
                        a, b = e_sum[:, :, :], e[:, n, :, :]
                    nc.gpsimd.tensor_tensor(e_sum[:, :, :], a, b, ALU.add).then_inc(pool_done.sem, 1)

                if on(t, -1):
                    add_e(1, 3)
                    pool.wait_ge(h_loaded.sem, h_loaded.after("x_again", t - 1))
                    hh = h[nxt]
                    nc.gpsimd.tensor_tensor(hh[:, :, :], hh[:, :, :], bo_row[:, :].unsqueeze(1).broadcast_to([P, NT, D]),
                                            ALU.add).then_inc(pool_done.sem, 1)
                if on(t, 1):
                    pool.wait_ge(dve_done.sem, dve_done.after("mask", t))
                    pool.nop(nofuse=True)
                    nc.gpsimd.affine_select(out=mask_diag[nxt], in_=mask_diag[nxt], compare_op=ALU.not_equal, fill=0.0, base=0,
                                            pattern=[[0, NT], [-1, P]], channel_multiplier=1).then_inc(pool_done.sem, 1)
                if on(t, 0):
                    add_e(0, 1)
                    add_e(0, 2)
                if on(t, -1):
                    pool.wait_ge(dve_done.sem, dve_done.after("var_eps", t))
                    nc.gpsimd.tensor_tensor(rstd[:, :], var_eps[:, :], minus_half[:, :], ALU.pow).then_inc(pool_done.sem, 1)
                if on(t, 0):
                    add_e(0, 3)
                if on(t, -1):
                    pool.wait_ge(adj_loaded.sem, adj_loaded.after("adj_again", t))
                    pool.nop(nofuse=True)
                    nc.gpsimd.tensor_scalar(adj_in[:, :, :], adj_in[:, :, :], -1.0, -NEG_INF, ALU.add, ALU.mult)\
                        .then_inc(pool_done.sem, 1)
                if on(t, 0):
                    add_e(1, 1)
                if on(t, -1):
                    pool.wait_ge(pe_done.sem, pe_done.after("ht1", t))
                    hh = h[nxt]
                    nc.gpsimd.tensor_tensor(hh[:, :, :], hh[:, :, :], fcb_row[:, :].unsqueeze(1).broadcast_to([P, NT, D]),
                                            ALU.add).then_inc(pool_done.sem, 1)
                if on(t, 0):
                    add_e(1, 2)

            program(pool, iteration)


_INS = ["x", "adj", "L0_gnn_Wq", "L0_gnn_bq", "L0_gnn_Wk", "L0_gnn_bk", "L0_gnn_Wv", "L0_gnn_bv", "L0_gnn_Wo",
        "L0_gnn_bo", "L0_gnn_gamma", "L0_gnn_beta", "L1_gnn_fc_w", "L1_gnn_fc_b", "L1_gnn_q_w", "L1_gnn_q_b",
        "L1_gnn_k_w", "L1_gnn_k_b"]


def kernel(**inputs):
    import numpy as _np
    import concourse.bacc as _bacc
    from concourse import mybir as _mybir
    from concourse.bass_utils import run_bass_kernel_spmd as _run

    nc = _bacc.Bacc("TRN2", target_bir_lowering=False, num_devices=1)
    arrays, args = {}, []
    for name in _INS:
        a = _np.ascontiguousarray(inputs[name])
        arrays[f"in_{name}"] = a
        args.append(nc.dram_tensor(f"in_{name}", a.shape, _mybir.dt.from_np(a.dtype), kind="ExternalInput").ap())
    args.append(nc.dram_tensor("out_y", (NB, N, D), F32, kind="ExternalOutput").ap())
    build(nc, *args)
    r = _run(nc, [arrays], core_ids=[0])
    return r.results[0]["out_y"]
```

```python
from contextlib import ExitStack

import concourse.bass as bass
from concourse import mybir

F32 = mybir.dt.float32
F32R = mybir.dt.float32r
BF16 = mybir.dt.bfloat16
ALU = mybir.AluOpType
ACT = mybir.ActivationFunctionType
AX = mybir.AxisListType

P = 128
NB, N, D = 16, 512, 256
NH, DH = 8, 32
GH = P // DH
NG = NH // GH
NT = N // P
DT = D // P
POS = NG * NT * GH
SCALE = float(DH) ** -0.5
BIG = 2.0 ** 100
NEG_INF = -1e9
SLOPE = 0.01
EPS = 1e-5
LOWEST = -3.0e38
STACK = 3 * DH
LEAD = 20

FIRST, LOOP_FROM, LOOP_TO, LAST = -1, 4, 14, NB + 1


def on(t, off):
    return not isinstance(t, int) or 0 <= t + off < NB


class Signal:

    def __init__(self, sem, steps, by=1):
        self.sem, self.by = sem, by
        self.place = {name: n for n, (name, _) in enumerate(steps)}
        self.offs = [off for _, off in steps]
        assert len(self.place) == len(steps)

    def after(self, step, t):
        last = self.place[step]
        if isinstance(t, int):
            return self.by * sum(min(max(t + off + (n <= last), 0), NB) for n, off in enumerate(self.offs))
        return t * (self.by * len(self.offs)) + self.by * sum(off + (n <= last) for n, off in enumerate(self.offs))


PE_STEPS = [
    (0, "xt0", 1), (0, "v1", 0), (1, "xt1", 1), (2, "pv0", -1), (3, "et0", -2), (3, "m4", 0), (4, "q0", 1),
    (5, "et1", -2), (5, "k0", 1), (6, "et2", -2), (6, "pv1", 0), (7, "m5", 0), (7, "sum1", -1), (8, "et3", -2),
    (9, "m6", 0), (10, "pv2", 0), (10, "at0", -2), (12, "at1", -2), (13, "op0", -1), (14, "m7", 0),
    (14, "pv3", 0), (15, "op1", -1), (16, "q1", 1), (18, "k1", 1), (18, "m0", 1), (18, "pv4", 0),
    (20, "mt0", 1), (21, "sum0", 0), (22, "m1", 1), (22, "pv5", 0), (22, "ht0", -1), (23, "ht1", -1),
    (25, "mt1", 1), (25, "m2", 1), (26, "pv6", 0), (26, "fc0", -1), (27, "fc1", -1), (28, "kb", -1),
    (29, "v0", 1), (30, "m3", 1), (30, "pv7", 0)]
OFF = {name: off for _, name, off in PE_STEPS}
FILLS = [name for _, name, _ in PE_STEPS if not name.startswith("pv")]
READ_BY = {
    "xt0": ("dve", "x_lo0"), "xt1": ("dve", "x_lo1"), "q0": ("dve", "q_lo0"), "k0": ("dve", "k_lo0"),
    "q1": ("dve", "q_lo1"), "k1": ("dve", "k_lo1"), "v0": ("act", "v0"), "v1": ("act", "v1"),
    "mt0": ("act", "mt0"), "mt1": ("act", "mt1"), "sum0": ("act", "sum0"), "sum1": ("act", "sum1"),
    "op0": ("dve", "h_add0"), "op1": ("dve", "h_add1"), "ht0": ("dve", "h_lo0"), "ht1": ("dve", "h_lo1"),
    "fc0": ("act", "feat0"), "fc1": ("act", "feat1"), "kb": ("dve", "l_max3"), "at0": ("dve", "fin0"),
    "at1": ("dve", "fin1"), **{f"et{c}": ("act", f"et{c}") for c in range(NT)},
    **{f"m{j}": ("dve", f"m{j}") for j in range(NH)}}
ACT_STEPS = [
    ("lexp0", -2), ("x_hi0", 1), ("lexp1", -2), ("x_hi1", 1), ("v1", 0), ("lexp2", -2), ("et0", -2), ("o_raw1", -1),
    ("lexp3", -2), ("q_hi0", 1), ("k_hi0", 1), ("et1", -2), ("et2", -2), ("sum1", -1), ("et3", -2),
    ("o_hi0", -1), ("o_hi1", -1), ("q_hi1", 1), ("k_hi1", 1), ("o_raw0", 0), ("mt0", 1), ("sum0", 0),
    ("h_hi0", -1), ("h_hi1", -1), ("mt1", 1), ("feat0", -1), ("feat1", -1), ("v0", 1), ("logit0", -1), ("logit1", -1),
    ("logit2", -1), ("logit3", -1)]
DVE_STEPS = [
    ("leaky1", -2), ("x_lo0", 1), ("leaky2", -2), ("x_lo1", 1), ("leaky3", -2), ("m4", 0),
    ("q_lo0", 1), ("k_lo0", 1), ("recip0", -1), ("mask", 1), ("m5", 0), ("recip1", -1), ("o_norm0", -1),
    ("o_norm1", -1), ("o_lo0", -1), ("o_lo1", -1), ("m6", 0), ("l_recip", -2),
    ("fin0", -2), ("fin1", -2), ("h_add0", -1), ("m7", 0), ("stats_a", -1), ("h_add1", -1), ("stats_b", -1),
    ("moments", -1), ("var_eps", -1), ("centre", -1), ("q_lo1", 1), ("m0", 1), ("k_lo1", 1), ("h_a", -1), ("h_b", -1),
    ("m1", 1), ("h_lo0", -1), ("h_lo1", -1), ("m2", 1), ("q_dot0", -1),
    ("q_dot1", -1), ("q_bias", -1), ("l_max1", -1), ("l_max3", -1), ("m3", 1), ("l_z", -1),
    ("l_nz", -1), ("l_negmax", -1), ("leaky0", -1)]
POOL_STEPS = [
    ("sum1_3", -1), ("x_bo", -1), ("diag", 1), ("sum0_1", 0), ("sum0_2", 0), ("sum0_3", 0), ("rstd", -1),
    ("l_mask", -1), ("sum1_1", 0), ("h_fcb", -1), ("sum1_2", 0)]


def maxima_tile(s):
    n = s - (POS - LEAD) if s >= POS - LEAD else s + LEAD
    return (1 if s >= POS - LEAD else 0), n // NT, n % NT


def build(nc, x, adj, wq, bq, wk, bk, wv, bv, wo, bo, gamma, beta, fc_w, fc_b, q_w, q_b, k_w, k_b, out):
    with ExitStack() as ctx:
        def sb(name, shape, dt=F32):
            return ctx.enter_context(nc.sbuf_tensor(name, shape, dt))

        def sem(name):
            return ctx.enter_context(nc.semaphore(name))

        weight_hi = sb("weight_hi", [P, 5, DT, D], F32R)
        weight_lo = sb("weight_lo", [P, 5, DT, D], F32R)
        WQ, WK, WV, WO, FC = range(5)
        uk_hi = sb("uk_hi", [P, DT, P], F32R)
        uk_lo = sb("uk_lo", [P, DT, P], F32R)
        bias_col = sb("bias_col", [P, 3, NG])
        gamma_row = sb("gamma_row", [P, D])
        beta_row = sb("beta_row", [P, D])
        bo_row = sb("bo_row", [P, D])
        fcb_row = sb("fcb_row", [P, D])
        qw_row = sb("qw_row", [P, D])
        kw_col = sb("kw_col", [P, DT])
        qkb = sb("qkb", [P, 2])
        logit_bias = sb("logit_bias", [P, 4])
        ident = sb("ident", [P, P])
        ident_b = sb("ident_b", [P, P], BF16)
        ones = sb("ones", [P, DH])
        minus_half = sb("minus_half", [P, NT])
        x_in = sb("x_in", [P, NT, D])
        adj_in = sb("adj_in", [P, NT, N])
        masks = sb("masks", [P, (2 * NT + 1) * N], BF16)
        mask = [masks[:, i * NT * N:(i + 1) * NT * N] for i in range(2)]
        mask_diag = [masks[:, i * NT * N:i * NT * N + NT * (N + P)].rearrange("p (c n) -> p c n", c=NT)[:, :, 0:P]
                     for i in range(2)]
        mask_t = [sb(f"mask_t{i}", [P, NT, N], BF16) for i in range(2)]
        xt_hi = sb("xt_hi", [P, DT, N], F32R)
        xt_lo = sb("xt_lo", [P, DT, N], F32R)
        qt_hi = [sb(f"qt_hi{g}", [P, N], F32R) for g in range(NG)]
        qt_lo = [sb(f"qt_lo{g}", [P, N], F32R) for g in range(NG)]
        kt_hi = [sb(f"kt_hi{g}", [P, N], F32R) for g in range(NG)]
        kt_lo = [sb(f"kt_lo{g}", [P, N], F32R) for g in range(NG)]
        q_stack = [sb(f"q_stack{g}", [STACK + 1, GH, N], F32R) for g in range(NG)]
        k_stack = [sb(f"k_stack{g}", [STACK + 1, GH, N], F32R) for g in range(NG)]
        v = sb("v", [P, NT, D])
        row_max = sb("row_max", [P, NH, NT])
        neg_max = sb("neg_max", [NT, 2, P], F32R)
        e = sb("e", [P, NT, GH, N])
        e_sum = sb("e_sum", [P, GH, N])
        o_hi = sb("o_hi", [P, NG, N], F32R)
        o_lo = sb("o_lo", [P, NG, N], F32R)
        o_raw = [sb("o_raw0", [P, N]), x_in[:, 2:4, :].rearrange("p c d -> p (c d)")]
        recip = [sb("recip0", [P, N]), x_in[:, 0:2, :].rearrange("p c d -> p (c d)")]
        h = [sb(f"h{i}", [P, NT, D]) for i in range(2)]
        stats = sb("stats", [P, NT, 6])
        moments = sb("moments", [P, NT, 2])
        var_eps = sb("var_eps", [P, NT])
        rstd = sb("rstd", [P, NT])
        ht_hi = sb("ht_hi", [P, DT, N], F32R)
        ht_lo = sb("ht_lo", [P, DT, N], F32R)
        feat = sb("feat", [P, NT, D])
        z = sb("z", [P, NT, N])
        zt = sb("zt", [P, NT, N])
        q_dot = sb("q_dot", [P, NT])
        q_bias = sb("q_bias", [P, NT])
        l_max = sb("l_max", [P, NT])
        l_z = sb("l_z", [P, NT])
        l_nz = sb("l_nz", [P, NT])
        l_negmax = sb("l_negmax", [P, NT])
        l_sum = sb("l_sum", [P, NT])
        l_recip = sb("l_recip", [P, NT])

        def pb(name):
            return ctx.enter_context(nc.psum_tensor(name, [P, 512], F32))
        st_bank = [pb("st_bank0"), pb("st_bank1")]
        sm_bank = [pb("sm_bank0"), pb("sm_bank1")]
        o_bank = pb("o_bank")
        shared = [pb(f"shared{i}") for i in range(3)]
        bank_of = {name: shared[n % 3] for n, name in enumerate(FILLS)}
        before = {name: (FILLS[n - 3], n < 3) for n, name in enumerate(FILLS)}

        tiles = [(s, 0) for s in range(POS)]
        st_done = Signal(sem("st_done"), tiles)
        exp_done = Signal(sem("exp_done"), tiles)
        sm_tiles = [(s, maxima_tile(s)[0]) for s in range(POS)]
        sm_done = Signal(sem("sm_done"), sm_tiles)
        max_done = Signal(sem("max_done"), sm_tiles)
        pe_done = Signal(sem("pe_done"), [(name, off) for _, name, off in PE_STEPS])
        act_done = Signal(sem("act_done"), ACT_STEPS)
        dve_done = Signal(sem("dve_done"), DVE_STEPS)
        pool_done = Signal(sem("pool_done"), POOL_STEPS)
        made = {"act": act_done, "dve": dve_done}
        adj_loaded = Signal(sem("adj_loaded"), [("adj", 1), ("adj_again", -1)], 16)
        x_loaded = Signal(sem("x_loaded"), [("x", 2)], 16)
        h_loaded = Signal(sem("h_loaded"), [("x_again", 0)], 16)
        stacked = [Signal(sem("stacked0"), [("g0", 1)], 16 * 6 * GH), Signal(sem("stacked1"), [("g1", 0)], 16 * 6 * GH)]
        max_placed = [Signal(sem(f"max_placed{i}"), [("g1", 0), ("g0", 1)], 16) for i in range(GH)]
        stored = [Signal(sem(f"stored{i}"), [("out", -2)], 16) for i in range(2)]
        weights_loaded, const_loaded = sem("weights_loaded"), sem("const_loaded")
        N_WEIGHTS, N_CONST = 6, 11
        ident_made = sem("ident_made")
        setup_pe, setup_act, setup_dve = sem("setup_pe"), sem("setup_act"), sem("setup_dve")

        def f(ap):
            return ap.bitcast(F32)

        def rows(dram, b, c0=0, c1=NT):
            return dram[bass.ds(b, 1), c0 * P:c1 * P, :].rearrange("a (c p) d -> p (a c) d", p=P)

        block = ctx.enter_context(nc.Block())

        def program(engine, iteration):
            for t in range(FIRST, LOOP_FROM):
                iteration(t, t % 2)
            with engine.Fori(LOOP_FROM // 2, LOOP_TO // 2) as pair:
                iteration(2 * pair, 0)
                iteration(2 * pair + 1, 1)
            for t in range(LOOP_TO, LAST + 1):
                iteration(t, t % 2)

        @block.sync
        def _(sp):
            for k, w in enumerate((wq, wk, wv, wo)):
                sp.dma_start(z[:, k, :].rearrange("p (o i) -> p o i", o=DT),
                             w.rearrange("(o p) i -> p o i", p=P)).then_inc(weights_loaded, 16)
            sp.dma_start(h[0][:, 0:DT, :], fc_w.rearrange("(o p) i -> p o i", p=P)).then_inc(weights_loaded, 16)
            sp.dma_start(kw_col[:, :], k_w.rearrange("a (g p) -> p (a g)", p=P),
                         allow_slow_non_contiguous=True).then_inc(weights_loaded, 16)
            sp.dma_start(x_in[:, :, :], rows(x, 0)).then_inc(x_loaded.sem, 16)
            for k, b in enumerate((bq, bk, bv)):
                sp.dma_start(bias_col[:, k, :], b.rearrange("(g p) -> p g", p=P),
                             allow_slow_non_contiguous=True).then_inc(const_loaded, 16)
            sp.dma_start(adj_in[:, :, :], rows(adj, 0)).then_inc(adj_loaded.sem, 16)
            for row, b in ((gamma_row, gamma), (beta_row, beta), (bo_row, bo), (fcb_row, fc_b)):
                sp.dma_start(row[:, :], b.partition_broadcast(P)).then_inc(const_loaded, 16)
            for row, b in ((qw_row[:, :], q_w), (zt[:, 2, 0:D], k_w)):
                sp.dma_start(row, b.rearrange("a d -> (a d)").partition_broadcast(P)).then_inc(const_loaded, 16)
            for k, b in enumerate((q_b, k_b)):
                sp.dma_start(qkb[:, k:k + 1], b.partition_broadcast(P)).then_inc(const_loaded, 16)

            def stack(g, t):
                sp.wait_ge(dve_done.sem, dve_done.after(f"k_lo{g}", t if g == 0 else t - 1))
                sp.nop(nofuse=True)
                for i in range(GH):
                    r = slice(DH * i, DH * (i + 1))
                    for part, (q_part, k_part) in enumerate(((qt_hi, kt_hi), (qt_lo, kt_hi), (qt_hi, kt_lo))):
                        to = slice(DH * part, DH * (part + 1))
                        sp.dma_start(f(q_stack[g][to, i, :]), f(q_part[g][r, :])).then_inc(stacked[g].sem, 16)
                        sp.dma_start(f(k_stack[g][to, i, :]), f(k_part[g][r, :])).then_inc(stacked[g].sem, 16)

            def place_max(j, t):
                g, i = j // GH, j % GH
                sp.wait_ge(dve_done.sem, dve_done.after(f"m{j}", t))
                sp.nop(nofuse=True)
                sp.dma_start(f(q_stack[g][STACK:STACK + 1, i, :]), f(neg_max[:, j % 2, :])).then_inc(max_placed[i].sem, 16)

            def iteration(t, par):
                if on(t, 1) and not (isinstance(t, int) and t == FIRST):
                    sp.wait_ge(dve_done.sem, dve_done.after("l_max3", t - 1))
                    sp.nop(nofuse=True)
                    sp.dma_start(adj_in[:, :, :], rows(adj, t + 1)).then_inc(adj_loaded.sem, 16)
                if on(t, 0):
                    sp.wait_ge(st_done.sem, st_done.after(POS - 1, t - 1))
                    sp.nop(nofuse=True)
                    stack(1, t)
                    place_max(4, t)
                    place_max(5, t)
                if on(t, -1):
                    sp.wait_ge(pool_done.sem, pool_done.after("diag", t))
                    sp.nop(nofuse=True)
                    sp.wait_ge(dve_done.sem, dve_done.after("l_max3", t - 1))
                    sp.nop(nofuse=True)
                    sp.dma_start(adj_in[:, :, :], rows(adj, t - 1)).then_inc(adj_loaded.sem, 16)
                if on(t, 0):
                    place_max(6, t)
                for half in range(2):
                    if on(t, -2):
                        sp.wait_ge(dve_done.sem, dve_done.after(f"fin{half}", t))
                        sp.nop(nofuse=True)
                        c = 2 * half
                        sp.dma_start(rows(out, t - 2, c, c + 2), h[par][:, c:c + 2, :]).then_inc(stored[half].sem, 16)
                if on(t, 0):
                    place_max(7, t)
                if on(t, 1):
                    sp.wait_ge(st_done.sem, st_done.after(POS // 2 - 1, t))
                    sp.nop(nofuse=True)
                    stack(0, t)
                    place_max(0, t)
                if on(t, 0):
                    for half in range(2):
                        sp.wait_ge(stored[half].sem, stored[half].after("out", t))
                        sp.nop(nofuse=True)
                    sp.dma_start(h[par][:, :, :], rows(x, t)).then_inc(h_loaded.sem, 16)
                if on(t, 1):
                    place_max(1, t)
                    place_max(2, t)
                if on(t, 2):
                    sp.wait_ge(dve_done.sem, dve_done.after("o_lo1", t))
                    sp.nop(nofuse=True)
                    sp.wait_ge(pe_done.sem, pe_done.after("xt1", t))
                    sp.nop(nofuse=True)
                    sp.dma_start(x_in[:, :, :], rows(x, t + 2)).then_inc(x_loaded.sem, 16)
                if on(t, 1):
                    place_max(3, t)

            sp.wait_ge(setup_pe, 6)
            program(sp, iteration)
            for half in range(2):
                sp.wait_ge(stored[half].sem, stored[half].after("out", LAST))
                sp.nop(nofuse=True)

        @block.tensor
        def _(pe):
            pe.wait_ge(ident_made, 9)
            pe.wait_ge(weights_loaded, 16 * N_WEIGHTS)
            setup_banks = [*shared, *sm_bank, o_bank]
            for k in range(5):
                for i in range(DT):
                    for o in range(DT):
                        src = z[:, k, o * D + i * P:o * D + (i + 1) * P] if k < 4 else h[0][:, o, i * P:(i + 1) * P]
                        last = nc.tensor.transpose(setup_banks[k][:, (i * DT + o) * P:(i * DT + o + 1) * P],
                                                   src, ident[:, :])
                last.then_inc(setup_pe, 1)
            pe.wait_ge(setup_dve, 1)
            for i in range(DT):
                for o in range(DT):
                    last = nc.tensor.matmul(setup_banks[5][:, i * P:(i + 1) * P], h[0][:, o, i * P:(i + 1) * P],
                                            zt[:, 0, o * P:(o + 1) * P], start=(o == 0), stop=(o == DT - 1))
            last.then_inc(setup_pe, 1)
            pe.wait_ge(setup_dve, 7)

            def bank_read(name, t):
                other, tb = name, t
                while True:
                    other, earlier = before[other]
                    tb = tb - 1 if earlier else tb
                    if on(tb, OFF[other]) or tb < FIRST:
                        break
                who, reader = READ_BY[other]
                return made[who].sem, made[who].after(reader, tb)

            def three_terms(bank, terms, kts=DT):
                for kt in range(kts):
                    (ah, al), (bh, bl) = terms(kt)
                    for n, (a, b) in enumerate(((ah, bh), (ah, bl), (al, bh))):
                        last = nc.tensor.matmul(bank, a, b, start=(kt == 0 and n == 0), stop=(kt == kts - 1 and n == 2))
                return last

            def iteration(t, par):
                nxt = 1 - par

                def turn_x(kt):
                    if kt == 0:
                        pe.wait_ge(x_loaded.sem, x_loaded.after("x", t - 1))
                    pe.wait_ge(*bank_read(f"xt{kt}", t))
                    bank = bank_of[f"xt{kt}"]
                    for c in range(NT):
                        last = nc.tensor.transpose(bank[:, c * P:(c + 1) * P], x_in[:, c, kt * P:(kt + 1) * P], ident[:, :])
                    last.then_inc(pe_done.sem, 1)

                def project_qk(name, w, g):
                    pe.wait_ge(dve_done.sem, dve_done.after("x_lo1", t))
                    pe.wait_ge(*bank_read(f"{name}{g}", t))
                    bank = bank_of[f"{name}{g}"]
                    o = slice(g * P, (g + 1) * P)
                    three_terms(bank[:, :], lambda kt: ((weight_hi[:, w, kt, o], weight_lo[:, w, kt, o]),
                                                        (xt_hi[:, kt, :], xt_lo[:, kt, :]))).then_inc(pe_done.sem, 1)

                def rows_times(name, half, hi, lo, w):
                    pe.wait_ge(*bank_read(f"{name}{half}", t))
                    bank = bank_of[f"{name}{half}"]
                    for k in range(2):
                        n = slice((2 * half + k) * P, (2 * half + k + 1) * P)
                        last = three_terms(bank[:, k * D:(k + 1) * D],
                                           lambda kt: ((hi[:, kt, n], lo[:, kt, n]),
                                                       (weight_hi[:, w, kt, :], weight_lo[:, w, kt, :])))
                    last.then_inc(pe_done.sem, 1)

                def out_project(half):
                    if half == 0:
                        pe.wait_ge(dve_done.sem, dve_done.after("o_lo1", t))
                    rows_times("op", half, o_hi, o_lo, WO)

                def fc_project(half):
                    if half == 0:
                        pe.wait_ge(dve_done.sem, dve_done.after("h_lo1", t))
                    rows_times("fc", half, ht_hi, ht_lo, FC)

                def turn_mask(half):
                    if half == 0:
                        pe.wait_ge(pool_done.sem, pool_done.after("diag", t))
                    pe.wait_ge(*bank_read(f"mt{half}", t))
                    bank = bank_of[f"mt{half}"][:, :].bitcast(BF16)
                    for k in range(2):
                        for c in range(NT):
                            key = (2 * half + k) * P
                            last = nc.tensor.transpose(bank[:, k * N + c * P:k * N + (c + 1) * P],
                                                       mask[nxt][:, c * N + key:c * N + key + P], ident_b[:, :])
                    last.then_inc(pe_done.sem, 1)

                def turn_max(j):
                    last_tile = (NT * j + NT - 1 + POS - LEAD) % POS
                    pe.wait_ge(max_done.sem, max_done.after(last_tile, t - 1 if j == GH else t))
                    pe.wait_ge(*bank_read(f"m{j}", t))
                    bank = bank_of[f"m{j}"]
                    nc.tensor.transpose(bank[0:NT, 0:P], row_max[:, j, :], ident[:, :]).then_inc(pe_done.sem, 1)

                def times_v(k):
                    kt = (k - 1) % NT
                    g = 1 if k == 0 else (k - 1) // NT
                    pe.wait_ge(exp_done.sem, exp_done.after((4 * k - 1) % POS, t if k else t - 1))
                    if k == 1:
                        pe.wait_ge(act_done.sem, act_done.after("v1", t))
                    if kt == 0:
                        pe.wait_ge(act_done.sem, act_done.after(f"o_raw{1 - g}", t))
                    for i in range(GH):
                        o = g * P + i * DH
                        last = nc.tensor.matmul(o_bank[i * DH:(i + 1) * DH, :], v[:, kt, o:o + DH], e[:, kt, i, :],
                                                start=(kt == 0), stop=(kt == NT - 1))
                    last.then_inc(pe_done.sem, 1)

                def total(g):
                    pe.wait_ge(pool_done.sem, pool_done.after(f"sum{g}_3", t))
                    pe.wait_ge(*bank_read(f"sum{g}", t))
                    bank = bank_of[f"sum{g}"]
                    for i in range(GH):
                        last = nc.tensor.matmul(bank[i * DH:(i + 1) * DH, :], ones[:, :], e_sum[:, i, :], start=True, stop=True)
                    last.then_inc(pe_done.sem, 1)

                def turn_h(kt):
                    if kt == 0:
                        pe.wait_ge(dve_done.sem, dve_done.after("h_b", t))
                    pe.wait_ge(*bank_read(f"ht{kt}", t))
                    bank = bank_of[f"ht{kt}"]
                    for c in range(NT):
                        last = nc.tensor.transpose(bank[:, c * P:(c + 1) * P], h[nxt][:, c, kt * P:(kt + 1) * P], ident[:, :])
                    last.then_inc(pe_done.sem, 1)

                def key_logits():
                    pe.wait_ge(*bank_read("kb", t))
                    bank = bank_of["kb"]
                    three_terms(bank[:, :], lambda kt: ((uk_hi[:, kt, :], uk_lo[:, kt, :]),
                                                        (ht_hi[:, kt, :], ht_lo[:, kt, :]))).then_inc(pe_done.sem, 1)

                def turn_z(c):
                    pe.wait_ge(act_done.sem, act_done.after(f"lexp{c}", t))
                    pe.wait_ge(*bank_read(f"et{c}", t))
                    bank = bank_of[f"et{c}"]
                    for k in range(NT):
                        last = nc.tensor.transpose(bank[:, k * P:(k + 1) * P], z[:, c, k * P:(k + 1) * P], ident[:, :])
                    last.then_inc(pe_done.sem, 1)

                def attend(c):
                    half, k = c // 2, c % 2
                    if c == 0:
                        pe.wait_ge(act_done.sem, act_done.after("et3", t))
                    if k == 0:
                        pe.wait_ge(*bank_read(f"at{half}", t))
                    bank = bank_of[f"at{half}"]
                    for kt in range(NT):
                        last = nc.tensor.matmul(bank[:, k * D:(k + 1) * D], zt[:, kt, c * P:(c + 1) * P], feat[:, kt, :],
                                                start=(kt == 0), stop=(kt == NT - 1))
                    if k == 1:
                        last.then_inc(pe_done.sem, 1)

                for s in range(POS):
                    g, kt, i = s // (POS // 2), s // GH % NT, s % GH
                    if on(t, 0):
                        if kt == 0 and i == 0:
                            pe.wait_ge(stacked[g].sem, stacked[g].after(f"g{g}", t if g else t - 1))
                            if g == 0:
                                pe.wait_ge(act_done.sem, act_done.after("mt1", t - 1))
                        if kt == 0:
                            pe.wait_ge(max_placed[i].sem, max_placed[i].after(f"g{g}", t if g else t - 1))
                        pe.wait_ge(exp_done.sem, exp_done.after((s - 2) % POS, t if s >= 2 else t - 1))
                        bank = st_bank[s % 2]
                        nc.tensor.matmul(bank[:, :], k_stack[g][:, i, kt * P:(kt + 1) * P], q_stack[g][:, i, :],
                                         start=True, stop=False)
                        nc.tensor.matmul(bank[:, :], ident_b[:, :], mask_t[par][:, kt, :],
                                         start=False, stop=True).then_inc(st_done.sem, 1)
                    off, j, qt = maxima_tile(s)
                    if on(t, off):
                        if j % GH == 0 and qt == 0:
                            pe.wait_ge(act_done.sem, act_done.after(f"k_hi{j // GH}", t))
                        pe.wait_ge(max_done.sem, max_done.after((s - 2) % POS, t if s >= 2 else t - 1))
                        r = slice(DH * (j % GH), DH * (j % GH + 1))
                        nc.tensor.matmul(sm_bank[s % 2][:, :], qt_hi[j // GH][r, qt * P:(qt + 1) * P],
                                         kt_hi[j // GH][r, :], start=True, stop=True).then_inc(sm_done.sem, 1)
                    if s == 0:
                        if on(t, 1):
                            turn_x(0)
                        if on(t, 0):
                            rows_times("v", 1, xt_hi, xt_lo, WV)
                    if s == 1:
                        if on(t, 1):
                            turn_x(1)
                    if s == 2:
                        if on(t, -1):
                            times_v(0)
                    if s == 3:
                        if on(t, -2):
                            turn_z(0)
                        if on(t, 0):
                            turn_max(4)
                    if s == 4:
                        if on(t, 1):
                            project_qk("q", WQ, 0)
                    if s == 5:
                        if on(t, -2):
                            turn_z(1)
                        if on(t, 1):
                            project_qk("k", WK, 0)
                    if s == 6:
                        if on(t, -2):
                            turn_z(2)
                        if on(t, 0):
                            times_v(1)
                    if s == 7:
                        if on(t, 0):
                            turn_max(5)
                        if on(t, -1):
                            total(1)
                    if s == 8:
                        if on(t, -2):
                            turn_z(3)
                    if s == 9:
                        if on(t, 0):
                            turn_max(6)
                        if on(t, -2):
                            attend(0)
                    if s == 10:
                        if on(t, 0):
                            times_v(2)
                        if on(t, -2):
                            attend(1)
                    if s == 11:
                        if on(t, -2):
                            attend(2)
                    if s == 12:
                        if on(t, -2):
                            attend(3)
                    if s == 13:
                        if on(t, -1):
                            out_project(0)
                    if s == 14:
                        if on(t, 0):
                            turn_max(7)
                            times_v(3)
                    if s == 15:
                        if on(t, -1):
                            out_project(1)
                    if s == 16:
                        if on(t, 1):
                            project_qk("q", WQ, 1)
                    if s == 18:
                        if on(t, 1):
                            project_qk("k", WK, 1)
                            turn_max(0)
                        if on(t, 0):
                            times_v(4)
                    if s == 20:
                        if on(t, 1):
                            turn_mask(0)
                    if s == 21:
                        if on(t, 0):
                            total(0)
                    if s == 22:
                        if on(t, 1):
                            turn_max(1)
                        if on(t, 0):
                            times_v(5)
                        if on(t, -1):
                            turn_h(0)
                    if s == 23:
                        if on(t, -1):
                            turn_h(1)
                    if s == 25:
                        if on(t, 1):
                            turn_mask(1)
                            turn_max(2)
                    if s == 26:
                        if on(t, 0):
                            times_v(6)
                        if on(t, -1):
                            fc_project(0)
                    if s == 27:
                        if on(t, -1):
                            fc_project(1)
                    if s == 28:
                        if on(t, -1):
                            key_logits()
                    if s == 29:
                        if on(t, 1):
                            rows_times("v", 0, xt_hi, xt_lo, WV)
                    if s == 30:
                        if on(t, 1):
                            turn_max(3)
                        if on(t, 0):
                            times_v(7)

            program(pe, iteration)

        @block.scalar
        def _(act):
            for k in range(5):
                act.wait_ge(setup_pe, k + 1)
                bank = [*shared, *sm_bank][k]
                nc.scalar.copy(weight_hi[:, k, :, :], bank[:, :].rearrange("p (i o) -> p i o", i=DT)).then_inc(setup_act, 1)
            act.wait_ge(setup_pe, 6)
            nc.scalar.copy(uk_hi[:, :, :], o_bank[:, 0:DT * P].rearrange("p (i o) -> p i o", i=DT)).then_inc(setup_act, 1)
            act.wait_ge(const_loaded, 16 * N_CONST)

            def iteration(t, par):
                nxt = 1 - par

                def logits(c):
                    act.wait_ge(dve_done.sem, dve_done.after("l_max1" if c < 2 else "l_max3", t))
                    nc.scalar.activation(z[:, c, :], z[:, c, :], ACT.Identity, bias=q_bias[:, c:c + 1])\
                        .then_inc(act_done.sem, 1)

                def exponentials(c):
                    act.wait_ge(dve_done.sem, dve_done.after(f"leaky{c}", t - 1 if c == 0 else t))
                    nc.scalar.activation(z[:, c, :], z[:, c, :], ACT.Exp, bias=l_negmax[:, c:c + 1],
                                         accum_out=l_sum[:, c:c + 1]).then_inc(act_done.sem, 1)

                def copy(dst, name, bank_ap):
                    act.wait_ge(pe_done.sem, pe_done.after(name, t))
                    nc.scalar.copy(dst, bank_ap).then_inc(act_done.sem, 1)

                def turned_z(c):
                    copy(zt[:, :, c * P:(c + 1) * P], f"et{c}",
                         bank_of[f"et{c}"][:, :].rearrange("p (k n) -> p k n", k=NT))

                def values(half):
                    act.wait_ge(pe_done.sem, pe_done.after("pv6" if half == 0 else "pv0", t))
                    copy(v[:, 2 * half:2 * half + 2, :], f"v{half}",
                         bank_of[f"v{half}"][:, :].rearrange("p (k n) -> p k n", k=2))

                def turned_mask(half):
                    copy(mask_t[nxt][:, 2 * half:2 * half + 2, :], f"mt{half}",
                         bank_of[f"mt{half}"][:, :].bitcast(BF16).rearrange("p (k n) -> p k n", k=2))

                def qk_high(name, dst, k, g):
                    act.wait_ge(pe_done.sem, pe_done.after(f"{name}{g}", t))
                    act.wait_ge(stacked[g].sem, stacked[g].after(f"g{g}", t - 1 if g == 0 else t))
                    nc.scalar.activation(dst[g][:, :], bank_of[f"{name}{g}"][:, :], ACT.Identity,
                                         bias=bias_col[:, k, g:g + 1]).then_inc(act_done.sem, 1)

                def o_high(g):
                    act.wait_ge(dve_done.sem, dve_done.after(f"o_norm{g}", t))
                    nc.scalar.activation(o_hi[:, g, :], o_raw[g][:, :], ACT.Identity,
                                         bias=bias_col[:, 2, g:g + 1]).then_inc(act_done.sem, 1)

                for s in range(POS):
                    g, kt, i = s // (POS // 2), s // GH % NT, s % GH
                    if on(t, 0):
                        act.wait_ge(st_done.sem, st_done.after(s, t))
                        if i == 0:
                            n = max(kt, 1)
                            if g == 1:
                                act.wait_ge(pe_done.sem, pe_done.after(f"pv{kt + 1}", t))
                                act.wait_ge(pool_done.sem, pool_done.after(f"sum0_{n}", t))
                            elif kt < NT - 1:
                                act.wait_ge(pe_done.sem, pe_done.after(f"pv{kt + 5}", t - 1))
                                act.wait_ge(pool_done.sem, pool_done.after(f"sum1_{n}", t - 1))
                            else:
                                act.wait_ge(pe_done.sem, pe_done.after("pv0", t))
                                act.wait_ge(pool_done.sem, pool_done.after("sum1_3", t))
                        nc.scalar.activation(e[:, kt, i, :], st_bank[s % 2][:, :], ACT.Exp, scale=SCALE)\
                            .then_inc(exp_done.sem, 1)
                    if s == 0 and on(t, -2):
                        exponentials(0)
                    if s in (1, 2) and on(t, 1):
                        if s == 1:
                            act.wait_ge(pe_done.sem, pe_done.after("v1", t))
                        copy(xt_hi[:, s - 1, :], f"xt{s - 1}", bank_of[f"xt{s - 1}"][:, :])
                    if s == 1 and on(t, -2):
                        exponentials(1)
                    if s == 2 and on(t, 0):
                        values(1)
                    if s == 3 and on(t, -2):
                        exponentials(2)
                    if s == 4 and on(t, -2):
                        turned_z(0)
                    if s == 4 and on(t, -1):
                        copy(o_raw[1][:, :], "pv0", o_bank[:, :])
                    if s == 4 and on(t, -2):
                        exponentials(3)
                    if s == 5 and on(t, 1):
                        qk_high("q", qt_hi, 0, 0)
                    if s == 6 and on(t, 1):
                        qk_high("k", kt_hi, 1, 0)
                    if s == 6 and on(t, -2):
                        turned_z(1)
                    if s == 7 and on(t, -2):
                        turned_z(2)
                    if s == 7 and on(t, -1):
                        copy(recip[1][:, :], "sum1", bank_of["sum1"][:, :])
                    if s == 8 and on(t, -2):
                        turned_z(3)
                    if s == 10 and on(t, -1):
                        o_high(0)
                        o_high(1)
                    if s == 17 and on(t, 1):
                        qk_high("q", qt_hi, 0, 1)
                    if s == 18 and on(t, 1):
                        qk_high("k", kt_hi, 1, 1)
                    if s == 19 and on(t, 0):
                        copy(o_raw[0][:, :], "pv4", o_bank[:, :])
                    if s == 21 and on(t, 1):
                        turned_mask(0)
                    if s == 22 and on(t, 0):
                        copy(recip[0][:, :], "sum0", bank_of["sum0"][:, :])
                    if s in (23, 24) and on(t, -1):
                        copy(ht_hi[:, s - 23, :], f"ht{s - 23}", bank_of[f"ht{s - 23}"][:, :])
                    if s == 25 and on(t, 1):
                        turned_mask(1)
                    if s in (27, 28) and on(t, -1):
                        half = s - 27
                        copy(feat[:, 2 * half:2 * half + 2, :], f"fc{half}",
                             bank_of[f"fc{half}"][:, :].rearrange("p (k n) -> p k n", k=2))
                    if s == 30 and on(t, 1):
                        values(0)
                    if s in (30, 31) and on(t, -1):
                        logits(2 * (s - 30))
                        logits(2 * (s - 30) + 1)

            program(act, iteration)

        @block.vector
        def _(dve):
            dve.wait_ge(weights_loaded, 16 * N_WEIGHTS)
            dve.wait_ge(ident_made, 9)
            for o in range(DT):
                last = nc.vector.tensor_scalar(zt[:, 0, o * P:(o + 1) * P], zt[:, 1, 0:P], kw_col[:, o:o + 1], None, ALU.add)
            last.then_inc(setup_dve, 1)
            for k in range(6):
                dve.wait_ge(setup_act, k + 1)
                hi, lo = (weight_hi[:, k, :, :], weight_lo[:, k, :, :]) if k < 5 else (uk_hi[:, :, :], uk_lo[:, :, :])
                bank = [*shared, *sm_bank, o_bank][k][:, 0:512 if k < 5 else DT * P]
                nc.vector.tensor_tensor(lo, bank.rearrange("p (i o) -> p i o", i=DT), f(hi), ALU.subtract).then_inc(setup_dve, 1)
            dve.wait_ge(const_loaded, 16 * N_CONST)
            for k, row in enumerate((qw_row[:, :], zt[:, 2, 0:D])):
                last = nc.vector.tensor_tensor_reduce(zt[:, 3, k * D:(k + 1) * D], fcb_row[:, :], row, 1.0, 0.0, ALU.mult, ALU.add,
                                                      logit_bias[:, k:k + 1])
            last.then_inc(setup_dve, 1)
            dve.wait_ge(setup_dve, 8)
            nc.vector.tensor_tensor(logit_bias[:, 0:2], logit_bias[:, 0:2], qkb[:, :], ALU.add).then_inc(setup_dve, 1)
            dve.wait_ge(setup_dve, 9)
            nc.vector.tensor_tensor(logit_bias[:, 3:4], logit_bias[:, 0:1], logit_bias[:, 1:2], ALU.add).then_inc(setup_dve, 1)
            dve.wait_ge(setup_dve, 10)

            def iteration(t, par):
                nxt = 1 - par
                done = dve_done.sem

                def lo_part(dst, name, hi_ready, hi):
                    dve.wait_ge(act_done.sem, act_done.after(hi_ready, t))
                    nc.vector.tensor_tensor(dst, bank_of[name][:, :], f(hi), ALU.subtract).then_inc(done, 1)

                def qk_lo(name, g, k, dst, hi):
                    dve.wait_ge(act_done.sem, act_done.after(f"{name}_hi{g}", t))
                    nc.vector.scalar_tensor_tensor(dst[g][:, :], bank_of[f"{name}{g}"][:, :], bias_col[:, k, g:g + 1],
                                                   f(hi[g][:, :]), ALU.add, ALU.subtract).then_inc(done, 1)

                def negate_max(j):
                    dve.wait_ge(pe_done.sem, pe_done.after(f"m{j}", t))
                    i2, g2 = (j - 2) % GH, (j - 2) % NH // GH
                    tb = t - 1 if j in (4, 5) else t
                    dve.wait_ge(max_placed[i2].sem, max_placed[i2].after(f"g{g2}", tb))
                    nc.vector.tensor_scalar(neg_max[:, j % 2, :], bank_of[f"m{j}"][0:NT, 0:P], -1.0, None, ALU.mult)\
                        .then_inc(done, 1)

                def reciprocals(g, quarters):
                    if quarters[0] == 0:
                        dve.wait_ge(act_done.sem, act_done.after(f"sum{g}", t if g else t - 1))
                    for k in quarters:
                        n = slice(k * P, (k + 1) * P)
                        last = nc.vector.reciprocal(recip[g][:, n], recip[g][:, n])
                    if quarters[-1] == NT - 1:
                        last.then_inc(done, 1)

                def normalise(g):
                    dve.wait_ge(act_done.sem, act_done.after(f"o_raw{g}", t if g else t - 1))
                    dve.wait_ge(dve_done.sem, dve_done.after(f"recip{g}", t))
                    nc.vector.tensor_tensor(o_raw[g][:, :], o_raw[g][:, :], recip[g][:, :], ALU.mult).then_inc(done, 1)

                def o_low(g):
                    dve.wait_ge(act_done.sem, act_done.after(f"o_hi{g}", t))
                    nc.vector.scalar_tensor_tensor(o_lo[:, g, :], o_raw[g][:, :], bias_col[:, 2, g:g + 1], f(o_hi[:, g, :]),
                                                   ALU.add, ALU.subtract).then_inc(done, 1)

                def finish(half):
                    dve.wait_ge(pe_done.sem, pe_done.after(f"at{half}", t))
                    if half == 0:
                        dve.wait_ge(dve_done.sem, dve_done.after("l_recip", t))
                    for k in range(2):
                        c = 2 * half + k
                        last = nc.vector.scalar_tensor_tensor(h[par][:, c, :], bank_of[f"at{half}"][:, k * D:(k + 1) * D],
                                                              l_recip[:, c:c + 1], h[par][:, c, :], ALU.mult, ALU.add)
                    last.then_inc(done, 1)

                def add_residual(half):
                    dve.wait_ge(pe_done.sem, pe_done.after(f"op{half}", t))
                    if half == 0:
                        dve.wait_ge(pool_done.sem, pool_done.after("x_bo", t))
                    hc = h[nxt][:, 2 * half:2 * half + 2, :]
                    nc.vector.tensor_tensor(hc, bank_of[f"op{half}"][:, :].rearrange("p (k n) -> p k n", k=2), hc, ALU.add)\
                        .then_inc(done, 1)

                def statistics(half):
                    dve.wait_ge(dve_done.sem, dve_done.after(f"h_add{half}", t))
                    for c in range(2 * half, 2 * half + 2):
                        last = nc.vector.bn_stats(stats[:, c, :], h[nxt][:, c, :])
                    last.then_inc(done, 1)

                def query_logits(half):
                    dve.wait_ge(act_done.sem, act_done.after(f"feat{half}", t))
                    if half == 0:
                        dve.wait_ge(pe_done.sem, pe_done.after("et3", t))
                    for k in range(2):
                        c = 2 * half + k
                        last = nc.vector.tensor_tensor_reduce(z[:, c, 0:D], feat[:, c, :], qw_row[:, :], 1.0, 0.0,
                                                              ALU.mult, ALU.add, q_dot[:, c:c + 1])
                    last.then_inc(done, 1)

                def leaky(c):
                    dve.wait_ge(act_done.sem, act_done.after(f"logit{c}", t if c == 0 else t - 1))
                    nc.vector.scalar_tensor_tensor(z[:, c, :], z[:, c, :], SLOPE, z[:, c, :], ALU.mult, ALU.max)\
                        .then_inc(done, 1)

                def layer1_maxima(half):
                    if half == 0:
                        dve.wait_ge(pe_done.sem, pe_done.after("kb", t))
                        dve.wait_ge(pool_done.sem, pool_done.after("l_mask", t))
                        dve.nop(nofuse=True)
                    for k in range(2):
                        c = 2 * half + k
                        last = nc.vector.tensor_tensor_reduce(z[:, c, :], bank_of["kb"][:, :], adj_in[:, c, :], 1.0, LOWEST,
                                                              ALU.add, ALU.max, l_max[:, c:c + 1])
                    last.then_inc(done, 1)

                for s in range(POS):
                    off, j, qt = maxima_tile(s)
                    if on(t, off):
                        if off == 1 and j == 0 and qt == 0:
                            dve.wait_ge(pool_done.sem, pool_done.after("diag", t))
                        dve.wait_ge(sm_done.sem, sm_done.after(s, t))
                        dve.nop(nofuse=True)
                        nc.vector.tensor_tensor_reduce(sm_bank[s % 2][:, :], sm_bank[s % 2][:, :],
                                                       mask[nxt if off else par][:, qt * N:(qt + 1) * N], 1.0, LOWEST,
                                                       ALU.add, ALU.max, row_max[:, j, qt:qt + 1]).then_inc(max_done.sem, 1)
                    if s in (1, 2) and on(t, 1):
                        lo_part(xt_lo[:, s - 1, :], f"xt{s - 1}", f"x_hi{s - 1}", xt_hi[:, s - 1, :])
                    if s in (0, 1, 2) and on(t, -2):
                        leaky(s + 1)
                    if s == 4 and on(t, 0):
                        negate_max(4)
                    if s == 5 and on(t, 1):
                        qk_lo("q", 0, 0, qt_lo, qt_hi)
                    if s == 6 and on(t, 1):
                        qk_lo("k", 0, 1, kt_lo, kt_hi)
                    if s in (3, 4, 5, 6) and on(t, -1):
                        reciprocals(0, (s - 3,))
                    if s == 7 and on(t, 1):
                        dve.wait_ge(adj_loaded.sem, adj_loaded.after("adj", t))
                        nc.vector.tensor_scalar(mask[nxt], adj_in[:, :, :].rearrange("p c n -> p (c n)"),
                                                0.0, -BIG, ALU.is_le, ALU.mult).then_inc(done, 1)
                    if s == 7 and on(t, 0):
                        negate_max(5)
                    if s in (8, 9) and on(t, -1):
                        reciprocals(1, (0, 1) if s == 8 else (2, 3))
                    if s == 10 and on(t, -1):
                        normalise(0)
                        normalise(1)
                    if s == 11 and on(t, -1):
                        o_low(0)
                        o_low(1)
                    if s == 11 and on(t, 0):
                        negate_max(6)
                    if s == 12 and on(t, -2):
                        dve.wait_ge(act_done.sem, act_done.after("lexp3", t))
                        nc.vector.reciprocal(l_recip[:, :], l_sum[:, :]).then_inc(done, 1)
                        dve.wait_ge(pool_done.sem, pool_done.after("h_fcb", t - 1))
                        finish(0)
                    if s == 13 and on(t, -2):
                        finish(1)
                    if s == 14 and on(t, -1):
                        add_residual(0)
                    if s == 15 and on(t, 0):
                        negate_max(7)
                    if s == 15 and on(t, -1):
                        statistics(0)
                    if s == 16 and on(t, -1):
                        add_residual(1)
                        statistics(1)
                    if s == 17 and on(t, -1):
                        dve.wait_ge(dve_done.sem, dve_done.after("stats_b", t))
                        dve.nop(nofuse=True)
                        for c in range(NT):
                            last = nc.vector.bn_aggr(moments[:, c, :], stats[:, c, :])
                        last.then_inc(done, 1)
                        dve.wait_ge(dve_done.sem, dve_done.after("moments", t))
                        nc.vector.tensor_scalar(var_eps[:, :], moments[:, :, 1], EPS, None, ALU.add).then_inc(done, 1)
                        for c in range(NT):
                            last = nc.vector.scalar_tensor_tensor(h[nxt][:, c, :], h[nxt][:, c, :], moments[:, c, 0:1],
                                                                  gamma_row[:, :], ALU.subtract, ALU.mult)
                        last.then_inc(done, 1)
                    if s == 18 and on(t, 1):
                        qk_lo("q", 1, 0, qt_lo, qt_hi)
                    if s == 19 and on(t, 1):
                        negate_max(0)
                        qk_lo("k", 1, 1, kt_lo, kt_hi)
                    if s in (20, 21) and on(t, -1):
                        if s == 20:
                            dve.wait_ge(pool_done.sem, pool_done.after("rstd", t))
                            dve.wait_ge(dve_done.sem, dve_done.after("centre", t))
                        for c in range(2 * (s - 20), 2 * (s - 20) + 2):
                            last = nc.vector.scalar_tensor_tensor(h[nxt][:, c, :], h[nxt][:, c, :], rstd[:, c:c + 1],
                                                                  beta_row[:, :], ALU.mult, ALU.add)
                        last.then_inc(done, 1)
                    if s == 23 and on(t, 1):
                        negate_max(1)
                    if s in (23, 24) and on(t, -1):
                        lo_part(ht_lo[:, s - 23, :], f"ht{s - 23}", f"h_hi{s - 23}", ht_hi[:, s - 23, :])
                    if s == 26 and on(t, 1):
                        negate_max(2)
                    if s == 27 and on(t, -1):
                        query_logits(0)
                    if s == 28 and on(t, -1):
                        query_logits(1)
                        dve.wait_ge(dve_done.sem, dve_done.after("q_dot1", t))
                        nc.vector.tensor_scalar(q_bias[:, :], q_dot[:, :], logit_bias[:, 3:4], None, ALU.add).then_inc(done, 1)
                    if s == 29 and on(t, -1):
                        layer1_maxima(0)
                    if s == 30 and on(t, -1):
                        layer1_maxima(1)
                    if s == 31 and on(t, 1):
                        negate_max(3)
                    if s == 31 and on(t, -1):
                        dve.wait_ge(dve_done.sem, dve_done.after("l_max3", t))
                        nc.vector.tensor_tensor(l_z[:, :], l_max[:, :], q_bias[:, :], ALU.add).then_inc(done, 1)
                        dve.wait_ge(dve_done.sem, dve_done.after("l_z", t))
                        nc.vector.tensor_scalar(l_nz[:, :], l_z[:, :], -1.0, None, ALU.mult).then_inc(done, 1)
                        dve.wait_ge(dve_done.sem, dve_done.after("l_nz", t))
                        nc.vector.scalar_tensor_tensor(l_negmax[:, :], l_nz[:, :], SLOPE, l_nz[:, :], ALU.mult, ALU.min)\
                            .then_inc(done, 1)
                        leaky(0)

            program(dve, iteration)

        @block.gpsimd
        def _(pool):
            for ap in (ident, ident_b):
                nc.gpsimd.memset(ap[:, :], 0.0).then_inc(ident_made, 1)
            pool.wait_ge(ident_made, 2)
            for ap in (ident, ident_b):
                nc.gpsimd.affine_select(out=ap[:, :], in_=ap[:, :], compare_op=ALU.not_equal, fill=1.0, base=0,
                                        pattern=[[-1, P]], channel_multiplier=1).then_inc(ident_made, 1)
            for n, (ap, value) in enumerate((*((f(k_stack[g][STACK:STACK + 1, :, :]), 1.0) for g in range(NG)),
                                             (minus_half[:, :], -0.5), (zt[:, 1, 0:P], 0.0), (ones[:, :], 1.0))):
                pool.wait_ge(ident_made, 4 + n)
                nc.gpsimd.memset(ap, value).then_inc(ident_made, 1)
            pool.wait_ge(const_loaded, 16 * N_CONST)

            def iteration(t, par):
                nxt = 1 - par

                def add_e(g, n):
                    slot = (g * NT + n) * GH + GH - 1
                    tb = t if (g, n) != (1, 3) else t - 1
                    pool.wait_ge(exp_done.sem, exp_done.after(slot, tb))
                    if n == 1:
                        pool.wait_ge(pe_done.sem, pe_done.after(f"sum{1 - g}", t))
                        a, b = e[:, 0, :, :], e[:, 1, :, :]
                    else:
                        pool.wait_ge(pool_done.sem, pool_done.after(f"sum{g}_{n - 1}", tb))
                        a, b = e_sum[:, :, :], e[:, n, :, :]
                    nc.gpsimd.tensor_tensor(e_sum[:, :, :], a, b, ALU.add).then_inc(pool_done.sem, 1)

                if on(t, -1):
                    add_e(1, 3)
                    pool.wait_ge(h_loaded.sem, h_loaded.after("x_again", t - 1))
                    hh = h[nxt]
                    nc.gpsimd.tensor_tensor(hh[:, :, :], hh[:, :, :], bo_row[:, :].unsqueeze(1).broadcast_to([P, NT, D]),
                                            ALU.add).then_inc(pool_done.sem, 1)
                if on(t, 1):
                    pool.wait_ge(dve_done.sem, dve_done.after("mask", t))
                    pool.nop(nofuse=True)
                    nc.gpsimd.affine_select(out=mask_diag[nxt], in_=mask_diag[nxt], compare_op=ALU.not_equal, fill=0.0, base=0,
                                            pattern=[[0, NT], [-1, P]], channel_multiplier=1).then_inc(pool_done.sem, 1)
                if on(t, 0):
                    add_e(0, 1)
                    add_e(0, 2)
                if on(t, 0):
                    add_e(0, 3)
                if on(t, -1):
                    pool.wait_ge(dve_done.sem, dve_done.after("var_eps", t))
                    nc.gpsimd.tensor_tensor(rstd[:, :], var_eps[:, :], minus_half[:, :], ALU.pow).then_inc(pool_done.sem, 1)
                if on(t, -1):
                    pool.wait_ge(adj_loaded.sem, adj_loaded.after("adj_again", t))
                    pool.nop(nofuse=True)
                    nc.gpsimd.tensor_scalar(adj_in[:, :, :], adj_in[:, :, :], -1.0, -NEG_INF, ALU.add, ALU.mult)\
                        .then_inc(pool_done.sem, 1)
                if on(t, 0):
                    add_e(1, 1)
                if on(t, -1):
                    pool.wait_ge(pe_done.sem, pe_done.after("ht1", t))
                    hh = h[nxt]
                    nc.gpsimd.tensor_tensor(hh[:, :, :], hh[:, :, :], fcb_row[:, :].unsqueeze(1).broadcast_to([P, NT, D]),
                                            ALU.add).then_inc(pool_done.sem, 1)
                if on(t, 0):
                    add_e(1, 2)

            program(pool, iteration)


_INS = ["x", "adj", "L0_gnn_Wq", "L0_gnn_bq", "L0_gnn_Wk", "L0_gnn_bk", "L0_gnn_Wv", "L0_gnn_bv", "L0_gnn_Wo",
        "L0_gnn_bo", "L0_gnn_gamma", "L0_gnn_beta", "L1_gnn_fc_w", "L1_gnn_fc_b", "L1_gnn_q_w", "L1_gnn_q_b",
        "L1_gnn_k_w", "L1_gnn_k_b"]


def kernel(**inputs):
    import numpy as _np
    import concourse.bacc as _bacc
    from concourse import mybir as _mybir
    from concourse.bass_utils import run_bass_kernel_spmd as _run

    nc = _bacc.Bacc("TRN2", target_bir_lowering=False, num_devices=1)
    arrays, args = {}, []
    for name in _INS:
        a = _np.ascontiguousarray(inputs[name])
        arrays[f"in_{name}"] = a
        args.append(nc.dram_tensor(f"in_{name}", a.shape, _mybir.dt.from_np(a.dtype), kind="ExternalInput").ap())
    args.append(nc.dram_tensor("out_y", (NB, N, D), F32, kind="ExternalOutput").ap())
    build(nc, *args)
    r = _run(nc, [arrays], core_ids=[0])
    return r.results[0]["out_y"]
```
